# Optimizing a Trainium2 kernel written in Bass

```python
import numpy as np
import jax
import jax.numpy as jnp

def _softmax(x, axis=-1):
    return jax.nn.softmax(x, axis=axis)
def _gelu(x):
    return jax.nn.gelu(x, approximate=True)
def _silu(x):
    return jax.nn.silu(x)
def _sigmoid(x):
    return jax.nn.sigmoid(x)
def _layernorm(x, axis=-1, eps=1e-5):
    m = jnp.mean(x, axis=axis, keepdims=True)
    v = jnp.var(x, axis=axis, keepdims=True)
    return (x - m) / jnp.sqrt(v + eps)
def _scatter_add(tgt, idx, src, axis=0):
    return tgt.at[idx].add(src)
def _segment_sum(src, seg, n):
    return jax.ops.segment_sum(src, seg, n)

kernel_name = 'mk_conv_seq_d1_conv_nchw128_775097'

def setup_inputs(seed: int = 0):
    np.random.seed(seed)
    _w = jnp.asarray
    def _rec_inputs():
        import jax
        import jax.numpy as jnp
        _gk = jax.random.key(seed)
        x = 7.22e-05 + 1 * jax.random.normal(jax.random.fold_in(_gk, 1), (4, 128, 128, 128), jnp.float32)
        return x
    x = _rec_inputs()
    def _L0_conv_setup():
        import jax, jax.numpy as jnp
        import numpy as np
        from jax import lax
        B, C, H, W = (4, 128, 128, 128)
        DG = 2
        K = 9
        EPS = 1e-05

        def conv2d(x, w, stride=1, pad=1):
            return lax.conv_general_dilated(x, w, (stride, stride), [(pad, pad), (pad, pad)], dimension_numbers=('NCHW', 'OIHW', 'NCHW'))

        def bn(x, p):
            g, b, m, v = (p[0], p[1], p[2], p[3])
            inv = g / jnp.sqrt(v + EPS)
            return x * inv[:, None, None] + (b - m * inv)[:, None, None]

        def deform_sample(x, py, px):
            Bb, Cc, Hh, Ww = x.shape
            Cg = Cc // DG
            xg = x.reshape(Bb, DG, Cg, Hh * Ww)
            y0 = jnp.floor(py)
            x0 = jnp.floor(px)
            fy = py - y0
            fx = px - x0
            y0i = y0.astype(jnp.int32)
            x0i = x0.astype(jnp.int32)

            def corner(yi, xi, wgt):
                valid = (yi >= 0) & (yi < Hh) & (xi >= 0) & (xi < Ww)
                idx = (jnp.clip(yi, 0, Hh - 1) * Ww + jnp.clip(xi, 0, Ww - 1)).reshape(Bb, DG, -1)
                v = jnp.take_along_axis(xg, idx[:, :, None, :], axis=3)
                return v * (wgt * valid).reshape(Bb, DG, 1, -1)
            val = corner(y0i, x0i, (1 - fy) * (1 - fx)) + corner(y0i, x0i + 1, (1 - fy) * fx) + corner(y0i + 1, x0i, fy * (1 - fx)) + corner(y0i + 1, x0i + 1, fy * fx)
            return val.reshape(Bb, DG, Cg, K, Hh, Ww)

        def modulated_deform_conv(x, off_w, off_b, dc_w, dc_b):
            Bb, Cc, Hh, Ww = x.shape
            off_out = conv2d(x, off_w) + off_b[None, :, None, None]
            o = off_out[:, :2 * DG * K].reshape(Bb, DG, K, 2, Hh, Ww)
            mask = jax.nn.sigmoid(off_out[:, 2 * DG * K:]).reshape(Bb, DG, K, Hh, Ww)
            ky = (jnp.arange(K) // 3 - 1).astype(x.dtype)
            kx = (jnp.arange(K) % 3 - 1).astype(x.dtype)
            iy = jnp.arange(Hh, dtype=x.dtype)[:, None]
            ix = jnp.arange(Ww, dtype=x.dtype)[None, :]
            py = o[:, :, :, 0] + iy + ky[None, None, :, None, None]
            px = o[:, :, :, 1] + ix + kx[None, None, :, None, None]
            g = deform_sample(x, py, px) * mask[:, :, None]
            wr = dc_w.reshape(dc_w.shape[0], DG, Cc // DG, K)
            out = jnp.einsum('odck,bdckhw->bohw', wr, g)
            return out + dc_b[None, :, None, None]
        key = jax.random.key(seed)
        ks = jax.random.split(key, 16)
        s3 = 1.0 / np.sqrt(C * 9)
        s1 = 1.0 / np.sqrt(C)

        def bn_params(k):
            k1, k2, k3, k4 = jax.random.split(k, 4)
            return jnp.stack([jax.random.uniform(k1, (C,)) + 0.5, jax.random.normal(k2, (C,)) * 0.1, jax.random.normal(k3, (C,)) * 0.1, jax.random.uniform(k4, (C,)) + 0.5])
        return {'x': jax.random.normal(ks[0], (B, C, H, W), jnp.float32), 'rb_w1': jax.random.normal(ks[1], (C, C, 3, 3), jnp.float32) * s3, 'rb_b1': jax.random.normal(ks[2], (C,), jnp.float32) * 0.01, 'rb_bn1': bn_params(ks[3]), 'rb_w2': jax.random.normal(ks[4], (C, C, 3, 3), jnp.float32) * s3, 'rb_b2': jax.random.normal(ks[5], (C,), jnp.float32) * 0.01, 'rb_bn2': bn_params(ks[6]), 'off_w': jax.random.normal(ks[7], (3 * DG * K, C, 3, 3), jnp.float32) * s3 * 0.1, 'off_b': jax.random.normal(ks[8], (3 * DG * K,), jnp.float32) * 0.01, 'dc_w': jax.random.normal(ks[9], (C, C, 3, 3), jnp.float32) * s3, 'dc_b': jax.random.normal(ks[10], (C,), jnp.float32) * 0.01, 'bn1': bn_params(ks[11]), 'cv2_w': jax.random.normal(ks[12], (C, C, 1, 1), jnp.float32) * s1, 'bn2': bn_params(ks[13])}
    _L0_conv_all = _L0_conv_setup()
    _L0_conv_in = {k: v for k, v in _L0_conv_all.items() if k in ('rb_w1', 'rb_b1', 'rb_bn1', 'rb_w2', 'rb_b2', 'rb_bn2', 'off_w', 'off_b', 'dc_w', 'dc_b', 'bn1', 'cv2_w', 'bn2', )}
    del _L0_conv_all

    return {
        "x": x,
        "L0_conv_rb_w1": _L0_conv_in["rb_w1"],
        "L0_conv_rb_b1": _L0_conv_in["rb_b1"],
        "L0_conv_rb_bn1": _L0_conv_in["rb_bn1"],
        "L0_conv_rb_w2": _L0_conv_in["rb_w2"],
        "L0_conv_rb_b2": _L0_conv_in["rb_b2"],
        "L0_conv_rb_bn2": _L0_conv_in["rb_bn2"],
        "L0_conv_off_w": _L0_conv_in["off_w"],
        "L0_conv_off_b": _L0_conv_in["off_b"],
        "L0_conv_dc_w": _L0_conv_in["dc_w"],
        "L0_conv_dc_b": _L0_conv_in["dc_b"],
        "L0_conv_bn1": _L0_conv_in["bn1"],
        "L0_conv_cv2_w": _L0_conv_in["cv2_w"],
        "L0_conv_bn2": _L0_conv_in["bn2"],
    }

def reference(x, L0_conv_rb_w1, L0_conv_rb_b1, L0_conv_rb_bn1, L0_conv_rb_w2, L0_conv_rb_b2, L0_conv_rb_bn2, L0_conv_off_w, L0_conv_off_b, L0_conv_dc_w, L0_conv_dc_b, L0_conv_bn1, L0_conv_cv2_w, L0_conv_bn2):
    import jax
    import jax.numpy as jnp
    def _L0_conv_ref(x, rb_w1, rb_b1, rb_bn1, rb_w2, rb_b2, rb_bn2, off_w, off_b, dc_w, dc_b, bn1, cv2_w, bn2):
        import jax, jax.numpy as jnp
        import numpy as np
        from jax import lax
        B, C, H, W = (4, 128, 128, 128)
        DG = 2
        K = 9
        EPS = 1e-05

        def conv2d(x, w, stride=1, pad=1):
            return lax.conv_general_dilated(x, w, (stride, stride), [(pad, pad), (pad, pad)], dimension_numbers=('NCHW', 'OIHW', 'NCHW'))

        def bn(x, p):
            g, b, m, v = (p[0], p[1], p[2], p[3])
            inv = g / jnp.sqrt(v + EPS)
            return x * inv[:, None, None] + (b - m * inv)[:, None, None]

        def deform_sample(x, py, px):
            Bb, Cc, Hh, Ww = x.shape
            Cg = Cc // DG
            xg = x.reshape(Bb, DG, Cg, Hh * Ww)
            y0 = jnp.floor(py)
            x0 = jnp.floor(px)
            fy = py - y0
            fx = px - x0
            y0i = y0.astype(jnp.int32)
            x0i = x0.astype(jnp.int32)

            def corner(yi, xi, wgt):
                valid = (yi >= 0) & (yi < Hh) & (xi >= 0) & (xi < Ww)
                idx = (jnp.clip(yi, 0, Hh - 1) * Ww + jnp.clip(xi, 0, Ww - 1)).reshape(Bb, DG, -1)
                v = jnp.take_along_axis(xg, idx[:, :, None, :], axis=3)
                return v * (wgt * valid).reshape(Bb, DG, 1, -1)
            val = corner(y0i, x0i, (1 - fy) * (1 - fx)) + corner(y0i, x0i + 1, (1 - fy) * fx) + corner(y0i + 1, x0i, fy * (1 - fx)) + corner(y0i + 1, x0i + 1, fy * fx)
            return val.reshape(Bb, DG, Cg, K, Hh, Ww)

        def modulated_deform_conv(x, off_w, off_b, dc_w, dc_b):
            Bb, Cc, Hh, Ww = x.shape
            off_out = conv2d(x, off_w) + off_b[None, :, None, None]
            o = off_out[:, :2 * DG * K].reshape(Bb, DG, K, 2, Hh, Ww)
            mask = jax.nn.sigmoid(off_out[:, 2 * DG * K:]).reshape(Bb, DG, K, Hh, Ww)
            ky = (jnp.arange(K) // 3 - 1).astype(x.dtype)
            kx = (jnp.arange(K) % 3 - 1).astype(x.dtype)
            iy = jnp.arange(Hh, dtype=x.dtype)[:, None]
            ix = jnp.arange(Ww, dtype=x.dtype)[None, :]
            py = o[:, :, :, 0] + iy + ky[None, None, :, None, None]
            px = o[:, :, :, 1] + ix + kx[None, None, :, None, None]
            g = deform_sample(x, py, px) * mask[:, :, None]
            wr = dc_w.reshape(dc_w.shape[0], DG, Cc // DG, K)
            out = jnp.einsum('odck,bdckhw->bohw', wr, g)
            return out + dc_b[None, :, None, None]
        h = jax.nn.relu(bn(conv2d(x, rb_w1) + rb_b1[None, :, None, None], rb_bn1))
        h = bn(conv2d(h, rb_w2) + rb_b2[None, :, None, None], rb_bn2)
        h = jax.nn.relu(h + x)
        h = modulated_deform_conv(h, off_w, off_b, dc_w, dc_b)
        h = jax.nn.leaky_relu(bn(h, bn1), 0.1)
        h = jax.nn.leaky_relu(bn(conv2d(h, cv2_w, pad=0), bn2), 0.1)
        return x + h

    def _gn(v, G=32, eps=1e-5):
        B_, C_, H_, W_ = v.shape
        g = v.reshape(B_, G, C_ // G, H_, W_)
        m = jnp.mean(g, axis=(2, 3, 4), keepdims=True)
        s = jnp.var(g, axis=(2, 3, 4), keepdims=True)
        return ((g - m) / jnp.sqrt(s + eps)).reshape(v.shape)

    def _ln_c(v, eps=1e-6):
        m = jnp.mean(v, axis=1, keepdims=True)
        s = jnp.var(v, axis=1, keepdims=True)
        return (v - m) / jnp.sqrt(s + eps)

    def _ln_t(v, eps=1e-5):
        m = jnp.mean(v, axis=-1, keepdims=True)
        s = jnp.var(v, axis=-1, keepdims=True)
        return (v - m) / jnp.sqrt(s + eps)

    def _to_tokens(v):
        B_, C_, H_, W_ = v.shape
        return v.reshape(B_, C_, H_ * W_).transpose(0, 2, 1)
    def _from_tokens(t, like):
        B_, C_, H_, W_ = like.shape
        return t.transpose(0, 2, 1).reshape(B_, C_, H_, W_)

    x = _L0_conv_ref(x, L0_conv_rb_w1, L0_conv_rb_b1, L0_conv_rb_bn1, L0_conv_rb_w2, L0_conv_rb_b2, L0_conv_rb_bn2, L0_conv_off_w, L0_conv_off_b, L0_conv_dc_w, L0_conv_dc_b, L0_conv_bn1, L0_conv_cv2_w, L0_conv_bn2)
    return x


_drawn_inputs = setup_inputs


def setup_inputs(seed=0):
    import zlib

    import numpy as np

    out = dict(_drawn_inputs(seed))
    spreads = {}
    factors = {'L0_conv_rb_b1': 37.938,
     'L0_conv_rb_b2': 25.285,
     'L0_conv_off_b': 8.0,
     'L0_conv_dc_b': 8.0}
    for name, (base, spread) in spreads.items():
        noise = np.random.default_rng([zlib.crc32(name.encode()), seed]).standard_normal(out[name].shape)
        drawn = base * np.exp(spread * noise) if base else spread * noise
        out[name] = jnp.asarray(drawn.astype(out[name].dtype))
    for name, factor in factors.items():
        out[name] = (out[name] * factor).astype(out[name].dtype)
    return out
```

```python
from contextlib import ExitStack

import numpy as np

import concourse.bass as bass
from concourse import mybir

ALU = mybir.AluOpType
ACT = mybir.ActivationFunctionType
AX = mybir.AxisListType
F32 = mybir.dt.float32
F32R = mybir.dt.float32r
F16 = mybir.dt.float16
I32 = mybir.dt.int32

C = 128
G = 2
CG = C // G
KS = 3
K = KS * KS
GK = G * K
EPS = 1e-5
SLOPE = 0.1
BANK = 512
MSCALE = 32768.0

ROWS = 4
PX = 12
QY, QX = ROWS + 4, PX + 4
assert QY * QX == 128
V_OY, V_M, V_OX = 0, GK, 2 * GK
NV = 3 * GK
HALF_V = 64
X_ROW = 64
DISP = (0, -1, 1)
NHAT = len(DISP)
YROWS = 2 * NHAT * GK
CROWS = 16


def constants(B, H, W):
    q = np.arange(128)
    qy, qx = q // QX, q % QX
    selx = np.zeros((128, GK, 128), np.float16)
    for g in range(G):
        for k in range(K):
            c = g * K + k
            selx[X_ROW + c, c] = 1
            selx[X_ROW + GK + c, c] = 1
            selx[0, c] = 1
            selx[1, c] = (k % KS) - 1 + 2 - qx
    sely = np.zeros((YROWS, GK, ROWS - 1 + QY, QX), np.float16)
    for c in range(GK):
        for d in range(NHAT):
            for part in range(2):
                sely[(part * NHAT + d) * GK + c, c, ROWS - 1 + 2 + (c % K) // KS - 1 + DISP[d]] = 1
    xpos = np.zeros((2, ROWS, W), np.float16)
    xpos[0] = np.arange(W) % PX
    xpos[1] = 1
    cols = np.zeros((128, 4), np.float32)
    for part in range(2):
        for d in range(NHAT):
            rows = slice((part * NHAT + d) * GK, (part * NHAT + d + 1) * GK)
            cols[rows, 0] = -DISP[d]
            cols[rows, 1] = -part
    cols[X_ROW + GK:X_ROW + 2 * GK, 2] = -1
    cols[0:GK, 3] = 1
    cols[X_ROW:X_ROW + 2 * GK, 3] = 1
    ch = np.arange(GK)
    taps = np.zeros((128, 3, GK), np.float32)
    taps[:, 0] = (ch % K) // KS - 1
    taps[:, 1] = (ch % K) % KS - 1
    taps[:, 2] = ch // K
    xcol = np.arange(128, dtype=np.float32)[:, None]
    rowpos = np.zeros((B * H, 128, 2), np.float32)
    rowpos[:, :, 0] = (np.arange(B * H) % H)[:, None]
    rowpos[:, :, 1] = (np.arange(B * H) // H * (H * W * G))[:, None]
    return dict(taps=taps, xcol=xcol, rowpos=rowpos, selx=selx, sely=sely, xpos=xpos, cols=cols, ident=np.eye(128, dtype=np.float32))




def at_least(engine, sem, value):
    if isinstance(value, int) and value <= 0:
        return
    engine.wait_ge(sem, value)


def batch_norm_columns(nc, chan, bn, work, sems):
    chan_loaded, bn_sqrt, bn_step, bn_ready = sems
    gamma, beta, mean, var, cbias = (chan[:, 4 * i:4 * i + 4] for i in range(5))
    a, s, r, t = (work[:, 4 * i:4 * i + 4] for i in range(4))

    def act_part(act):
        act.wait_ge(bn_step, 1)
        nc.scalar.activation(s, a, ACT.Sqrt).then_inc(bn_sqrt, 1)

    def dve_part(dve):
        n = [0]

        def step(instruction):
            n[0] += 1
            instruction.then_inc(bn_step, 1)
            dve.wait_ge(bn_step, n[0])

        dve.wait_ge(chan_loaded, 32)
        step(nc.vector.tensor_scalar(a, var, EPS, None, ALU.add))
        dve.wait_ge(bn_sqrt, 1)
        step(nc.vector.reciprocal(r, s))
        for _ in range(2):
            step(nc.vector.tensor_tensor(t, r, r, ALU.mult))
            step(nc.vector.tensor_tensor(t, t, a, ALU.mult))
            step(nc.vector.tensor_scalar(t, t, -0.5, 1.5, ALU.mult, ALU.add))
            step(nc.vector.tensor_tensor(r, r, t, ALU.mult))
        step(nc.vector.tensor_tensor(bn[:, 0:4], gamma, r, ALU.mult))
        step(nc.vector.tensor_tensor(t, mean, bn[:, 0:4], ALU.mult))
        step(nc.vector.tensor_tensor(s, cbias, bn[:, 0:4], ALU.mult))
        step(nc.vector.tensor_tensor(t, beta, t, ALU.subtract))
        step(nc.vector.tensor_tensor(bn[:, 4:8], t, s, ALU.add))
        step(nc.vector.tensor_scalar(bn[:, 8:9], bn[:, 2:3], 1.0 / MSCALE, None, ALU.mult))
        nc.vector.tensor_copy(work[:, 15:16], bn[:, 8:9]).then_inc(bn_ready, 1)

    return act_part, dve_part


def convolution_block(nc, B, H, W, xpad, chan_d, w1, w2, w3, w3_bias, h1pad, hpad, offsets, chan, bn, work):
    PER = H // CROWS
    NS = B * PER
    TURNS = NS // 2
    PAIRS = W // 2
    M = 4
    HALVES = 2
    HR = CROWS // HALVES
    ORDER = (2, 1, 0, 3)
    CONV1, CONV2, CONV3 = range(3)
    inputs, outputs = (xpad, h1pad, hpad), (h1pad, hpad, offsets)
    first_row = (0, 0, 1)
    out_row = (1, 2, 0)
    assert HR * PAIRS == BANK and B > 1 and 2 * HALF_V == C
    with ExitStack() as ctx:
        def sb(name, shape, dt=F32):
            return ctx.enter_context(nc.sbuf_tensor(name, shape, dt))

        def sem(name):
            return ctx.enter_context(nc.semaphore(name))

        w_raw = sb("w_raw", [C, KS, KS, C])
        w_ends = sb("w_ends", [C, KS, C])
        w_mixed = sb("w_mixed", [C, KS, M, C])
        w_hi = [sb(f"w_hi{c}", [C, KS, M, C], F32R) for c in range(2)]
        w_lo = [sb(f"w_lo{c}", [C, KS, M, C], F32R) for c in range(2)]
        bias3 = sb("bias3", [C, 1])
        rows_in = [sb(f"rows_in{p}", [C, CROWS + 2, W + 2]) for p in range(2)]
        exact = sb("exact", [C, M, CROWS + 2, PAIRS])
        in_hi = [sb(f"in_hi{p}", [C, M, CROWS + 2, PAIRS], F32R) for p in range(2)]
        in_lo = [sb(f"in_lo{p}", [C, M, CROWS + 2, PAIRS], F32R) for p in range(2)]
        x_res = [sb(f"x_res{p}", [C, HALVES, HR * W]) for p in range(2)]
        m2 = [sb(f"m2_{h}", [C, BANK]) for h in range(HALVES)]
        middle = sb("middle", [C, 2, BANK])
        summed = [sb(f"summed{h}", [C, HR * PAIRS, 2]) for h in range(HALVES)]
        rows_out = [sb(f"rows_out{h}", [C, HR * W]) for h in range(HALVES)]
        zeros = sb("zeros", [C, 2 * W])
        acc = [ctx.enter_context(nc.psum_tensor(f"acc{h}", [C, M, BANK], F32)) for h in range(HALVES)]

        chan_loaded, bn_sqrt, bn_step, bn_ready = (sem(n) for n in ("chan_loaded", "bn_sqrt", "bn_step", "bn_ready"))
        w_loaded, w_ends_ready, w_mixed_ready = sem("w_loaded"), sem("w_ends_ready"), sem("w_mixed_ready")
        w_hi_ready, w_lo_ready = sem("w_hi_ready"), sem("w_lo_ready")
        zeros_ready, zeros_stored, borders_zero = sem("zeros_ready"), sem("zeros_stored"), sem("borders_zero")
        rows_loaded = [sem(f"rows_loaded{p}") for p in range(2)]
        res_loaded = [sem(f"res_loaded{p}") for p in range(2)]
        transformed, hi_ready, lo_ready = sem("transformed"), sem("hi_ready"), sem("lo_ready")
        product_done, m2_ready, middle_ready, pair_ready = (
            sem(n) for n in ("product_done", "m2_ready", "middle_ready", "pair_ready"))
        sum_done, out_ready = sem("sum_done"), sem("out_ready")
        out_stored = [sem(f"out_stored{h}") for h in range(HALVES)]
        sp_passed, pool_passed = sem("sp_passed"), sem("pool_passed")
        bn_act, bn_dve = batch_norm_columns(nc, chan, bn, work, (chan_loaded, bn_sqrt, bn_step, bn_ready))
        block = ctx.enter_context(nc.Block())

        def fills_before(conv, s):
            if isinstance(s, int) and s < 0 and conv > 0:
                conv, s = conv - 1, s + NS
            return HALVES * (NS * conv + s) if conv < CONV3 else HALVES * NS * CONV3 + s

        def fills(conv):
            return HALVES if conv < CONV3 else 1

        def strips(engine, body):
            for conv in range(3):
                def turn(i):
                    for p in range(2):
                        body(conv, 2 * i + p, p)

                turn(0)
                if TURNS > 2:
                    with engine.Fori(1, TURNS - 1) as i:
                        turn(i)
                turn(TURNS - 1)

        def two_ahead(engine, prepare, results):
            def body(conv, s, p):
                def ahead():
                    if isinstance(s, int) and s + 2 >= NS:
                        if conv + 1 < CONV3:
                            prepare(conv + 1, s + 2 - NS, p)
                    elif conv < CONV3:
                        prepare(conv, s + 2, p)

                results(conv, s, p, ahead)

            prepare(CONV1, 0, 0)
            prepare(CONV1, 1, 1)
            strips(engine, body)

        @block.sync
        def _(sp):
            sp.dma_start(w_raw[:].rearrange("c y x o -> c (y x) o"), w1).then_inc(w_loaded, 16)

            def load(conv, s, p):
                b, y = s // PER, (s % PER) * CROWS
                if isinstance(s, int) and s == 0 and conv > 0:
                    sp.wait_ge(zeros_stored, 16 * 4 * B)
                if conv > 0:
                    for h in range(HALVES):
                        sp.wait_ge(out_stored[h], (conv - 1) * 16 * NS + (b + 1) * (16 * PER))
                        sp.sem_inc(sp_passed, 1)
                at_least(sp, transformed, M * (NS * conv + s - 1))
                sp.sem_inc(sp_passed, 1)
                sp.dma_start(rows_in[p][:, :, 1:W + 1], inputs[conv][b, :, bass.ds(y + first_row[conv], CROWS + 2), :]
                             ).then_inc(rows_loaded[p], 16)
                if conv == CONV2:
                    at_least(sp, sum_done, HALVES * (s - 1))
                    sp.sem_inc(sp_passed, 1)
                    sp.dma_start(x_res[p][:].rearrange("c h (r w) -> c (h r) w", w=W),
                                 xpad[b, :, bass.ds(y + 1, CROWS), :]).then_inc(res_loaded[p], 16)
                if isinstance(s, int) and s == 1 and conv < CONV3:
                    sp.wait_ge(w_mixed_ready, M * (conv + 1))
                    if conv == CONV1:
                        sp.dma_start(w_raw[:].rearrange("c y x o -> c (y x) o"), w2).then_inc(w_loaded, 16)
                    else:
                        sp.dma_start(w_raw[:, :, :, 0:HALF_V].rearrange("c y x o -> c (y x) o"), w3
                                     ).then_inc(w_loaded, 16)

            strips(sp, load)
            for h in range(HALVES):
                sp.wait_ge(out_stored[h], 16 * 2 * NS + 32 * TURNS)

        @block.gpsimd
        def _(pool):
            for p in range(2):
                for x in (0, W + 1):
                    nc.gpsimd.memset(rows_in[p][:, :, x:x + 1], 0.0).then_inc(borders_zero, 1)
            nc.gpsimd.memset(zeros[:], 0.0).then_inc(zeros_ready, 1)
            pool.wait_ge(borders_zero, 4)

            def transform(conv, s, p):
                n = NS * conv + s
                pairs = rows_in[p][:].rearrange("c r (i e) -> c r i e", e=2)
                d = [pairs[:, :, e // 2:e // 2 + PAIRS, e % 2] for e in range(4)]
                pool.wait_ge(rows_loaded[p], 16 * (s // 2 + 1 + TURNS * conv))
                for k, m in enumerate(ORDER):
                    if conv == CONV3 and not (isinstance(s, int) and s == 0):
                        pool.wait_ge(product_done, M * (fills_before(conv, s) - 1) + k + 1)
                    else:
                        at_least(pool, lo_ready, M * (n - 1) + k + 1)
                    pool.sem_inc(pool_passed, 1)
                    first, second, op = ((d[0], d[2], ALU.subtract), (d[1], d[2], ALU.add),
                                         (d[2], d[1], ALU.subtract), (d[1], d[3], ALU.subtract))[m]
                    nc.gpsimd.tensor_tensor(exact[:, m], first, second, op).then_inc(transformed, 1)

            strips(pool, transform)

        @block.tensor
        def _(pe):
            def convolve(conv, s, p):
                if isinstance(s, int) and s == 0:
                    pe.wait_ge(w_lo_ready, conv + 1)
                pe.wait_ge(lo_ready, M * (NS * conv + s + 1))
                for h in range(HALVES):
                    at_least(pe, pair_ready, 2 * (fills_before(conv, s) + h - 1))
                    for m in ORDER:
                        for dy in range(KS):
                            y = HR * h + dy
                            for part, (w, rows) in enumerate(((w_hi, in_hi), (w_hi, in_lo), (w_lo, in_hi))):
                                mm = nc.tensor.matmul(acc[h][:, m, :], w[conv][:, dy, m, :], rows[p][:, m, y:y + HR, :],
                                                      start=(dy == 0 and part == 0), stop=(dy == KS - 1 and part == 2))
                        mm.then_inc(product_done, 1)

            def convolve_h(s, p):
                if isinstance(s, int) and s == 0:
                    pe.wait_ge(w_mixed_ready, M * (CONV3 + 1))
                pe.wait_ge(pair_ready, 2 * (fills_before(CONV3, s) - 1))
                for k, m in enumerate(ORDER):
                    pe.wait_ge(transformed, M * (NS * CONV3 + s) + k + 1)
                    for dy in range(KS):
                        for h in range(HALVES):
                            y = HR * h + dy
                            mm = nc.tensor.matmul(acc[p][HALF_V * h:HALF_V * h + HALF_V, m, :],
                                                  w_mixed[:, dy, m, 0:HALF_V], exact[:, m, y:y + HR, :],
                                                  start=(dy == 0), stop=(dy == KS - 1))
                    mm.then_inc(product_done, 1)

            strips(pe, lambda conv, s, p: convolve(conv, s, p) if conv < CONV3 else convolve_h(s, p))

        @block.scalar
        def _(act):
            act.dma_start(chan[:], chan_d).then_inc(chan_loaded, 16)
            act.dma_start(bias3[:], w3_bias).then_inc(chan_loaded, 16)
            bn_act(act)
            act.wait_ge(bn_ready, 1)
            act.wait_ge(zeros_ready, 1)
            for b in range(B):
                for y in (0, H + 1):
                    act.dma_start(h1pad[b, :, y, :], zeros[:, 0:W]).then_inc(zeros_stored, 16)
                for y in (0, H + 2):
                    act.dma_start(hpad[b, :, y:y + 2, :], zeros[:].rearrange("c (r w) -> c r w", w=W)
                                  ).then_inc(zeros_stored, 16)

            def round_rows(conv, s, p):
                n = NS * conv + s
                for k, m in enumerate(ORDER):
                    act.wait_ge(transformed, M * n + k + 1)
                    if k == 0:
                        at_least(act, product_done, M * fills_before(conv, s - 1))
                    nc.scalar.copy(in_hi[p][:, m], exact[:, m]).then_inc(hi_ready, 1)

            def keep_m2(conv, s, p, f):
                h = f if conv < CONV3 else p
                n = fills_before(conv, s) + f
                act.wait_ge(product_done, M * n + 1)
                at_least(act, middle_ready, 2 * (n - 1))
                nc.scalar.copy(m2[h][:], acc[h][:, 2, :]).then_inc(m2_ready, 1)

            def store(conv, s, p, f):
                b, y = s // PER, (s % PER) * CROWS
                h = f if conv < CONV3 else p
                n = fills_before(conv, s) + f
                if conv < CONV3:
                    at_least(act, out_stored[h], 16 * (NS * conv + s))
                else:
                    act.wait_ge(out_stored[h], 16 * 2 * NS + 32 * (s // 2))
                pairs = summed[h][:].rearrange("c i e -> c (i e)")
                if conv == CONV1:
                    act.wait_ge(pair_ready, 2 * (n + 1))
                    nc.scalar.activation(rows_out[h][:], pairs, ACT.Relu, bias=bn[:, 4:5], scale=bn[:, 0:1]
                                         ).then_inc(out_ready, 1)
                elif conv == CONV2:
                    act.wait_ge(sum_done, HALVES * s + f + 1)
                    nc.scalar.activation(rows_out[h][:], pairs, ACT.Relu, bias=bn[:, 5:6]).then_inc(out_ready, 1)
                else:
                    act.wait_ge(pair_ready, 2 * (n + 1))
                    nc.scalar.activation(rows_out[h][:], pairs, ACT.Identity, bias=bias3[:]).then_inc(out_ready, 1)
                act.wait_ge(out_ready, n + 1)
                rows = rows_out[h][:].rearrange("c (r w) -> c r w", w=W)
                if conv < CONV3:
                    act.dma_start(outputs[conv][b, :, bass.ds(y + out_row[conv] + HR * f, HR), :], rows
                                  ).then_inc(out_stored[h], 16)
                else:
                    for z in range(HALVES):
                        act.dma_start(offsets[b, :, bass.ds(y + HR * z, HR), :], rows[HALF_V * z:HALF_V * z + NV]
                                      ).then_inc(out_stored[h], 16)

            def results(conv, s, p, ahead):
                for f in range(fills(conv)):
                    keep_m2(conv, s, p, f)
                for f in range(fills(conv)):
                    if f == fills(conv) - 1:
                        ahead()
                    store(conv, s, p, f)

            two_ahead(act, round_rows, results)

        @block.vector
        def _(dve):
            def mix_weights(conv):
                n = C if conv < CONV3 else HALF_V
                g = [w_raw[:, :, x, 0:n] for x in range(KS)]
                ends, mixed = w_ends[:, :, 0:n], w_mixed[:, :, :, 0:n]
                dve.wait_ge(w_loaded, 16 * (conv + 1))
                at_least(dve, w_lo_ready, conv)
                nc.vector.tensor_tensor(ends, g[0], g[2], ALU.add).then_inc(w_ends_ready, 1)
                dve.wait_ge(w_ends_ready, 2 * conv + 1)
                nc.vector.tensor_scalar(ends, ends, 0.5, None, ALU.mult).then_inc(w_ends_ready, 1)
                dve.wait_ge(w_ends_ready, 2 * conv + 2)
                for m, sign in ((1, 0.5), (2, -0.5)):
                    nc.vector.scalar_tensor_tensor(mixed[:, :, m, :], g[1], sign, ends, ALU.mult, ALU.add
                                                   ).then_inc(w_mixed_ready, 1)
                for m, x in ((0, 0), (3, 2)):
                    nc.vector.tensor_copy(mixed[:, :, m, :], g[x]).then_inc(w_mixed_ready, 1)
                dve.wait_ge(w_mixed_ready, M * (conv + 1))
                if conv < CONV3:
                    nc.vector.tensor_copy(w_hi[conv][:], mixed).then_inc(w_hi_ready, 1)
                    dve.wait_ge(w_hi_ready, conv + 1)
                    nc.vector.tensor_tensor(w_lo[conv][:], mixed, w_hi[conv][:].bitcast(F32), ALU.subtract
                                            ).then_inc(w_lo_ready, 1)

            def split_rows(conv, s, p):
                n = NS * conv + s
                for k, m in enumerate(ORDER):
                    dve.wait_ge(hi_ready, M * n + k + 1)
                    nc.vector.tensor_tensor(in_lo[p][:, m], exact[:, m], in_hi[p][:, m].bitcast(F32),
                                            ALU.subtract).then_inc(lo_ready, 1)
                if isinstance(s, int) and s == 1 and conv < CONV3:
                    mix_weights(conv + 1)

            def combine(conv, s, p, ahead):
                for f in range(fills(conv)):
                    h = f if conv < CONV3 else p
                    n = fills_before(conv, s) + f
                    dve.wait_ge(m2_ready, n + 1)
                    dve.wait_ge(product_done, M * n + 2)
                    at_least(dve, pair_ready, 2 * n)
                    for e, op in enumerate((ALU.add, ALU.subtract)):
                        nc.vector.tensor_tensor(middle[:, e, :], acc[h][:, 1, :], m2[h][:], op
                                                ).then_inc(middle_ready, 1)
                    dve.wait_ge(middle_ready, 2 * n + 1)
                    dve.wait_ge(product_done, M * n + 3)
                    at_least(dve, out_ready, n - 1)
                    nc.vector.tensor_tensor(summed[h][:, :, 0], acc[h][:, 0, :], middle[:, 0, :], ALU.add
                                            ).then_inc(pair_ready, 1)
                    dve.wait_ge(middle_ready, 2 * n + 2)
                    dve.wait_ge(product_done, M * n + 4)
                    nc.vector.tensor_tensor(summed[h][:, :, 1], middle[:, 1, :], acc[h][:, 3, :], ALU.subtract
                                            ).then_inc(pair_ready, 1)
                    if conv == CONV2:
                        pairs = summed[h][:].rearrange("c i e -> c (i e)")
                        dve.wait_ge(pair_ready, 2 * (n + 1))
                        dve.wait_ge(res_loaded[p], 16 * (s // 2 + 1))
                        nc.vector.scalar_tensor_tensor(pairs, pairs, bn[:, 1:2], x_res[p][:, h, :], ALU.mult, ALU.add
                                                       ).then_inc(sum_done, 1)
                ahead()

            mix_weights(CONV1)
            bn_dve(dve)
            dve.wait_ge(bn_ready, 1)
            two_ahead(dve, split_rows, combine)


def deformable_block(nc, B, H, W, xpad, hpad, offsets, out, tables, wd, wc, bn, is_large):
    PER = H // ROWS
    NS = B * PER
    N = ROWS * W
    assert N == BANK
    NP = -(-W // PX)
    HW2 = (NP + 1) * PX
    width = [min(PX, W - PX * i) for i in range(NP)]
    PSTEP = [range(a, b) for a, b in ((0, 1), (1, 3), (3, 5), (5, 7), (7, 9), (9, 11), (11, 11), (11, 11), (11, 11))]
    TR = [list(range(r * 4, min(r * 4 + 4, NP))) for r in range(-(-NP // 4))]
    NT = len(TR)
    TSTEP = {6: (0, 1), 7: (2,)}
    OSTEP = {6: range(0, 3), 7: range(3, 6), 8: range(6, 9)}
    assert max(j for j in range(K) if PSTEP[j]) < min(OSTEP) and NP % 2 == 1 and NT == 3
    V_LOADS = 16 * (2 * NHAT + 2 * NHAT + 2)
    with ExitStack() as ctx:
        def sb(name, shape, dt=F32):
            return ctx.enter_context(nc.sbuf_tensor(name, shape, dt))

        def sem(name):
            return ctx.enter_context(nc.semaphore(name))

        def psum(name, shape):
            return ctx.enter_context(nc.psum_tensor(name, shape, F32))

        selx = sb("selx", [128, GK, 128], F16)
        sely = sb("sely", [YROWS, GK, (ROWS - 1 + QY) * QX], F16)
        cols = sb("cols", [128, 4])
        ident = sb("ident", [128, 128])
        wdt = sb("wdt", [C, K, C])
        wct = sb("wct", [C, C])
        rows_h = [sb(f"rows_h{p}", [C, QY, HW2]) for p in range(2)]
        cut_rows = sb("cut_rows", [C, NP, QY, QX])
        patches = [sb(f"patches{p}", [128, NP, C]) for p in range(2)]
        vy = [sb(f"vy{p}", [YROWS, N]) for p in range(2)]
        vm = [sb(f"vm{p}", [YROWS, N]) for p in range(2)]
        vx = [sb(f"vx{p}", [128, N]) for p in range(2)]
        oabs = sb("oabs", [128, N])
        largest = sb("largest", [128, N])
        ox16 = sb("ox16", [128, N], F16)
        xrows = [sb(f"xrows{p}", [128, N], F16) for p in range(2)]
        yabs = sb("yabs", [YROWS, N])
        yhat = sb("yhat", [YROWS, N])
        mrep = sb("mrep", [YROWS, N])
        ywt = sb("ywt", [YROWS, N])
        ywt16 = sb("ywt16", [YROWS, N], F16)
        yrows = [sb(f"yrows{p}", [YROWS, N], F16) for p in range(2)]
        xabs = sb("xabs", [128, G, N])
        xhat = [sb(f"xhat{p}", [128, G, N]) for p in range(2)]
        A = [sb(f"A{p}", [128, K, G, N]) for p in range(2)]
        samples = sb("samples", [C, K, N])
        u = sb("u", [C, N])
        z = sb("z", [C, N])
        xres = [sb(f"xres{p}", [C, N]) for p in range(2)]
        vmax = sb("vmax", [128, 2])

        px = psum("px", [128, G, BANK])
        py = psum("py", [128, G, BANK])
        pg = [psum(f"pg{i}", [128, BANK]) for i in range(3)]
        po = psum("po", [128, BANK])

        names = """tables_loaded cleared cut ox16_ready xrows_ready oabs_ready yabs_ready yhat_ready mrep_ready
            largest_y largest_x turned patches_ready ywt_ready ywt16_ready yrows_ready vmax_ready xd_ready
            xabs_ready xhat_ready yb_ready a_ready sampled samples_ready contracted ulin_ready u_ready c1_done
            zlin_ready z_ready added large_ready large_counted""".split()
        (tables_loaded, cleared, cut, ox16_ready, xrows_ready, oabs_ready,
         yabs_ready, yhat_ready, mrep_ready, largest_y, largest_x, turned, patches_ready, ywt_ready, ywt16_ready, yrows_ready, vmax_ready, xd_ready, xabs_ready, xhat_ready, yb_ready, a_ready, sampled, samples_ready, contracted, ulin_ready, u_ready, c1_done, zlin_ready, z_ready, added, large_ready, large_counted) = (sem(n) for n in names)
        v_loaded = [sem(f"v_loaded{p}") for p in range(2)]
        h_loaded = [sem(f"h_loaded{p}") for p in range(2)]
        x_loaded = [sem(f"x_loaded{p}") for p in range(2)]
        out_stored = [sem(f"out_stored{p}") for p in range(2)]
        sp_passed, pool_passed = sem("d_sp_passed"), sem("d_pool_passed")
        block = ctx.enter_context(nc.Block())

        def pipeline(engine, iteration):
            def peeled(t):
                iteration(t, t % 2, t < NS, 1 <= t <= NS, 2 <= t <= NS + 1, 3 <= t <= NS + 2)

            for t in range(4):
                peeled(t)
            if NS > 4:
                with engine.Fori(2, NS // 2) as i:
                    for p in range(2):
                        iteration(2 * i + p, p, True, True, True, True)
            for t in range(NS, NS + 3):
                peeled(t)

        def strip(s):
            return s // PER, (s % PER) * ROWS

        @block.sync
        def _(sp):
            for dst, src in ((wdt[:], wd), (cols[:], tables["cols"]), (ident[:], tables["ident"]),
                             (wct[:], wc), (selx[:], tables["selx"]),
                             (sely[:], tables["sely"].rearrange("p c y x -> p c (y x)"))):
                sp.dma_start(dst, src).then_inc(tables_loaded, 16)
            sp.wait_ge(cleared, 1)
            for p in range(2):
                sp.dma_start(xrows[p][0:2, :], tables["xpos"]).then_inc(tables_loaded, 16)

            def iteration(t, p, prep, front, back, tail):
                if prep:
                    b, y = strip(t)
                    at_least(sp, cut, 2 * (t - 1))
                    sp.sem_inc(sp_passed, 1)
                    sp.dma_start(rows_h[p][:, :, 2:2 + W], hpad[b, :, bass.ds(y, QY), :]).then_inc(h_loaded[p], 16)
                    for used in (yabs_ready, mrep_ready, xrows_ready):
                        at_least(sp, used, t - 1)
                        sp.sem_inc(sp_passed, 1)
                    for tile, row, times in ((vy[p][:], V_OY, 2 * NHAT), (vm[p][:], V_M, 2 * NHAT),
                                             (vx[p][X_ROW:X_ROW + 2 * GK, :], V_OX, 2)):
                        for r in range(times):
                            sp.dma_start(tile[r * GK:r * GK + GK], offsets[b, row:row + GK, bass.ds(y, ROWS), :]
                                         .rearrange("c r w -> c (r w)")).then_inc(v_loaded[p], 16)
                if back:
                    b, y = strip(t - 2)
                    at_least(sp, out_stored[p], 16 * ((t - 2) // 2))
                    sp.sem_inc(sp_passed, 1)
                    sp.dma_start(xres[p][:].rearrange("c (r w) -> c r w", w=W),
                                 xpad[b, :, bass.ds(y + 1, ROWS), :]).then_inc(x_loaded[p], 16)

            pipeline(sp, iteration)

        @block.gpsimd
        def _(pool):
            for p in range(2):
                nc.gpsimd.memset(rows_h[p][:], 0.0)
                nc.gpsimd.memset(xrows[p][:], 0.0)
            nc.gpsimd.memset(largest[:], 0.0).then_inc(cleared, 1)
            pool.wait_ge(cleared, 1)

            def iteration(t, p, prep, front, back, tail):
                q = 1 - p
                if prep:
                    pool.wait_ge(h_loaded[p], 16 * (t // 2 + 1))
                    at_least(pool, turned, NT * t)
                    pool.sem_inc(pool_passed, 1)
                    nc.gpsimd.tensor_copy(cut_rows[:, :, :, 0:PX].rearrange("c i y x -> c y i x"),
                                          rows_h[p][:, :, 0:NP * PX].rearrange("c y (i x) -> c y i x", x=PX)
                                          ).then_inc(cut, 1)
                    nc.gpsimd.tensor_copy(cut_rows[:, :, :, PX:QX].rearrange("c i y x -> c y i x"),
                                          rows_h[p][:, :, PX:].rearrange("c y (i x) -> c y i x", x=PX)[:, :, :, 0:QX - PX]
                                          ).then_inc(cut, 1)
                if tail:
                    b, y = strip(t - 3)
                    pool.wait_ge(z_ready, t - 2)
                    pool.wait_ge(x_loaded[q], 16 * ((t - 3) // 2 + 1))
                    nc.gpsimd.tensor_tensor(xres[q][:], z[:], xres[q][:], ALU.add).then_inc(added, 1)
                    pool.wait_ge(added, t - 2)
                    pool.dma_start(out[b, :, bass.ds(y, ROWS), :],
                                   xres[q][:].rearrange("c (r w) -> c r w", w=W)).then_inc(out_stored[q], 16)

            pipeline(pool, iteration)
            for p in range(2):
                pool.wait_ge(out_stored[p], 16 * (NS // 2))

        @block.tensor
        def _(pe):
            pe.wait_ge(tables_loaded, 16 * 8)
            def iteration(t, p, prep, front, back, tail):
                q = 1 - p
                for j in range(K):
                    if front:
                        n = 9 * (t - 1) + j
                        if j == 0:
                            pe.wait_ge(xrows_ready, t)
                        at_least(pe, xabs_ready, n)
                        for g in range(G):
                            mm = nc.tensor.matmul(px[:, g, :], selx[:, g * K + j, :], xrows[q][:],
                                                  start=True, stop=True)
                        mm.then_inc(xd_ready, 1)
                    if back:
                        for i in PSTEP[j]:
                            if i == 0:
                                pe.wait_ge(a_ready, K * (t - 1))
                            if i < 3:
                                pe.wait_ge(patches_ready, NT * min(t, NS) if isinstance(t, int) else NT * t)
                            else:
                                pe.wait_ge(samples_ready, NP * (t - 2) + i - 2)
                            w = width[i]
                            for g in range(G):
                                mm = nc.tensor.matmul(
                                    pg[i % 3][CG * g:CG * g + CG, 0:K * ROWS * w],
                                    patches[p][:, i, CG * g:CG * g + CG],
                                    A[p][:, :, g, :].rearrange("q k (r x) -> q k r x", x=W)[:, :, :, PX * i:PX * i + w],
                                    start=True, stop=True)
                            mm.then_inc(sampled, 1)
                    if tail and j == 4:
                        pe.wait_ge(u_ready, t - 2)
                        nc.tensor.matmul(po[:], wct[:], u[:], start=True, stop=True).then_inc(c1_done, 1)
                    if prep:
                        for r in TSTEP.get(j, ()):
                            at_least(pe, samples_ready, NP * (t - 1) + r - 2)
                            pe.wait_ge(cut, 2 * (t + 1))
                            bank = pg[(NP + r) % 3]
                            for m, i in enumerate(TR[r]):
                                mm = nc.tensor.transpose(bank[:, m * C:m * C + C],
                                                         cut_rows[:, i].rearrange("c y x -> c (y x)"), ident[:])
                            mm.then_inc(turned, 1)
                    if back and j in OSTEP:
                        for k in OSTEP[j]:
                            if k == 0:
                                pe.wait_ge(samples_ready, NP * (t - 1))
                                at_least(pe, zlin_ready, t - 2)
                            mm = nc.tensor.matmul(po[:], wdt[:, k, :], samples[:, k, :], start=(k == 0),
                                                  stop=(k == K - 1))
                        if k == K - 1:
                            mm.then_inc(contracted, 1)
                    if front:
                        at_least(pe, a_ready, n)
                        if j == 0:
                            pe.wait_ge(yrows_ready, t)
                        for g in range(G):
                            for r in range(ROWS):
                                span = slice(r * W, r * W + W)
                                window = slice((ROWS - 1 - r) * QX, (ROWS - 1 - r) * QX + 128)
                                mm = nc.tensor.matmul(py[:, g, span], sely[:, g * K + j, window], yrows[q][:, span],
                                                      start=True, stop=True)
                        mm.then_inc(yb_ready, 1)

            pipeline(pe, iteration)
            pe.wait_ge(large_ready, 1)
            nc.tensor.matmul(po[0:1, 0:1], vmax[:, 1:2], cols[:, 3:4], start=True, stop=True).then_inc(large_counted, 1)

        @block.scalar
        def _(act):
            act.wait_ge(tables_loaded, 16 * 8)

            def iteration(t, p, prep, front, back, tail):
                q = 1 - p
                for j in range(K):
                    if front:
                        n = 9 * (t - 1) + j
                        h = (j + q) % 2
                        act.wait_ge(xd_ready, n + 1)
                        at_least(act, xhat_ready, n)
                        nc.scalar.activation(xabs[:], px[:], ACT.Abs).then_inc(xabs_ready, 1)
                        act.wait_ge(xabs_ready, n + 1)
                        at_least(act, a_ready, n - 1)
                        nc.scalar.activation(xhat[h][:], xabs[:], ACT.Relu, bias=1.0, scale=-1.0
                                             ).then_inc(xhat_ready, 1)
                    if tail and j == 0:
                        act.wait_ge(contracted, t - 2)
                        at_least(act, c1_done, t - 3)
                        nc.scalar.activation(u[:], po[:], ACT.Identity, bias=bn[:, 6:7], scale=bn[:, 8:9]
                                             ).then_inc(ulin_ready, 1)
                    if tail and j == 5:
                        act.wait_ge(c1_done, t - 2)
                        at_least(act, added, t - 3)
                        nc.scalar.activation(z[:], po[:], ACT.Identity, bias=bn[:, 7:8], scale=bn[:, 3:4]
                                             ).then_inc(zlin_ready, 1)
                    if prep:
                        if j == 5:
                            act.wait_ge(v_loaded[p], V_LOADS * (t // 2 + 1))
                            at_least(act, yhat_ready, t)
                            at_least(act, largest_y, t)
                            nc.scalar.activation(yabs[:], vy[p][:], ACT.Abs, bias=cols[0:YROWS, 0:1]
                                                 ).then_inc(yabs_ready, 1)
                            act.wait_ge(yabs_ready, t + 1)
                            at_least(act, ywt_ready, t)
                            nc.scalar.activation(yhat[:], yabs[:], ACT.Relu, bias=1.0, scale=-1.0
                                                 ).then_inc(yhat_ready, 1)
                        if j == 6:
                            nc.scalar.activation(mrep[:], vm[p][:], ACT.Sigmoid).then_inc(mrep_ready, 1)
                        if j == 7:
                            x_rows = slice(X_ROW, X_ROW + 2 * GK)
                            act.wait_ge(ox16_ready, t + 1)
                            at_least(act, largest_x, t)
                            nc.scalar.activation(oabs[x_rows, :], ox16[x_rows, :], ACT.Abs).then_inc(oabs_ready, 1)
                        for r in TSTEP.get(j, ()):
                            act.wait_ge(turned, NT * t + r + 1)
                            m = len(TR[r])
                            nc.scalar.copy(patches[p][:, 4 * r:4 * r + m, :],
                                           pg[(NP + r) % 3][:, 0:m * C].rearrange("q (m c) -> q m c", c=C)
                                           ).then_inc(patches_ready, 1)

            pipeline(act, iteration)

        @block.vector
        def _(dve):
            dve.wait_ge(tables_loaded, 16 * 8)
            dve.wait_ge(cleared, 1)

            def iteration(t, p, prep, front, back, tail):
                q = 1 - p
                for j in range(K):
                    if back:
                        for i in PSTEP[j]:
                            dve.wait_ge(sampled, NP * (t - 2) + i + 1)
                            if i == 0:
                                at_least(dve, contracted, t - 2)
                            w = width[i]
                            nc.vector.tensor_copy(
                                samples[:].rearrange("c k (r x) -> c k r x", x=W)[:, :, :, PX * i:PX * i + w],
                                pg[i % 3][:, 0:K * ROWS * w].rearrange("c (k r x) -> c k r x", k=K, x=w)
                            ).then_inc(samples_ready, 1)
                    if prep and j == 4:
                        ox = slice(X_ROW, X_ROW + 2 * GK)
                        dve.wait_ge(v_loaded[p], V_LOADS * (t // 2 + 1))
                        at_least(dve, xrows_ready, t)
                        at_least(dve, oabs_ready, t)
                        nc.vector.tensor_copy(ox16[ox, :], vx[p][ox, :]).then_inc(ox16_ready, 1)
                        dve.wait_ge(ox16_ready, t + 1)
                        at_least(dve, xd_ready, K * (t - 1))
                        nc.vector.scalar_tensor_tensor(xrows[p][ox, :], ox16[ox, :], cols[ox, 2:3], vx[p][ox, :],
                                                       ALU.mult, ALU.add).then_inc(xrows_ready, 1)
                    if prep and j == 6:
                        dve.wait_ge(yabs_ready, t + 1)
                        at_least(dve, largest_y, t)
                        nc.vector.tensor_tensor(largest[0:GK, :], largest[0:GK, :], yabs[0:GK, :], ALU.max
                                                ).then_inc(largest_y, 1)
                    if prep and j == 7:
                        dve.wait_ge(mrep_ready, t + 1)
                        dve.wait_ge(yhat_ready, t + 1)
                        at_least(dve, yrows_ready, t)
                        nc.vector.scalar_tensor_tensor(ywt[:], yhat[:], MSCALE, mrep[:], ALU.mult, ALU.mult
                                                       ).then_inc(ywt_ready, 1)
                        dve.wait_ge(ywt_ready, t + 1)
                        nc.vector.tensor_copy(ywt16[:], ywt[:]).then_inc(ywt16_ready, 1)
                        dve.wait_ge(ywt16_ready, t + 1)
                        at_least(dve, yb_ready, K * (t - 1))
                        nc.vector.scalar_tensor_tensor(yrows[p][:], ywt16[:], cols[0:YROWS, 1:2], ywt[:],
                                                       ALU.mult, ALU.add).then_inc(yrows_ready, 1)
                    if prep and j == 8:
                        dve.wait_ge(oabs_ready, t + 1)
                        at_least(dve, largest_x, t)
                        x_rows = slice(X_ROW, X_ROW + 2 * GK)
                        nc.vector.tensor_tensor(largest[x_rows, :], largest[x_rows, :], oabs[x_rows, :], ALU.max
                                                ).then_inc(largest_x, 1)
                    if front:
                        n = 9 * (t - 1) + j
                        h = (j + q) % 2
                        dve.wait_ge(xhat_ready, n + 1)
                        dve.wait_ge(yb_ready, n + 1)
                        if j == 0:
                            at_least(dve, sampled, NP * (t - 2))
                        nc.vector.tensor_tensor(A[q][:, j, :, :], xhat[h][:], py[:], ALU.mult).then_inc(a_ready, 1)
                    if tail and j == 0:
                        dve.wait_ge(ulin_ready, t - 2)
                        nc.vector.scalar_tensor_tensor(u[:], u[:], SLOPE, u[:], ALU.mult, ALU.max).then_inc(u_ready, 1)
                    if tail and j == 5:
                        dve.wait_ge(zlin_ready, t - 2)
                        nc.vector.scalar_tensor_tensor(z[:], z[:], SLOPE, z[:], ALU.mult, ALU.max).then_inc(z_ready, 1)

            pipeline(dve, iteration)
            dve.wait_ge(largest_x, NS)
            dve.wait_ge(largest_y, NS)
            nc.vector.tensor_reduce(vmax[:, 0:1], largest[:], AX.X, ALU.max).then_inc(vmax_ready, 1)
            dve.wait_ge(vmax_ready, 1)
            nc.vector.tensor_scalar(vmax[:, 1:2], vmax[:, 0:1], 1.0, None, ALU.is_ge).then_inc(large_ready, 1)
            dve.wait_ge(large_counted, 1)
            nc.vector.tensor_scalar(is_large[0:1, :], po[0:1, 0:1], 1.0, None, ALU.min).then_inc(large_ready, 1)
            dve.wait_ge(large_ready, 2)


def general_block(nc, B, H, W, xpad, hpad, hpix, out, tables, wo, wo_bias, wd, wc, bn, is_large):
    assert W == 128
    ROWS_ALL = B * H
    with ExitStack() as ctx:
        def sb(name, shape, dt=F32):
            return ctx.enter_context(nc.sbuf_tensor(f"g_{name}", shape, dt))

        def sem(name):
            return ctx.enter_context(nc.semaphore(f"g_{name}"))

        def psum(name, shape):
            return ctx.enter_context(nc.psum_tensor(f"g_{name}", shape, F32))

        ident = sb("ident", [128, 128])
        ones = sb("ones", [1, 128])
        bias_row = sb("bias_row", [1, 128])
        wot = sb("wot", [C, K, HALF_V])
        wdt = sb("wdt", [C, K, C])
        wct = sb("wct", [C, C])
        taps = sb("taps", [128, 3, GK])
        xcol = sb("xcol", [128, 1])
        hrow = sb("hrow", [C, W])
        hrow_t = sb("hrow_t", [W, C])
        rows_h = sb("rows_h", [C, KS, W + 2])
        xrow = sb("xrow", [C, W])
        rowpos = sb("rowpos", [128, 2])
        mask = sb("mask", [128, GK])
        whole = sb("whole", [128, 2, GK], I32)
        coord = sb("coord", [128, 2, GK])
        low = sb("low", [128, 2, GK])
        work = sb("work", [128, 2, GK])
        side = sb("side", [128, 2, 2, GK])
        place = sb("place", [128, 2, 2, GK])
        cweight = sb("cweight", [128, 4, GK])
        cindex_f = sb("cindex_f", [128, 4, GK])
        cindex = sb("cindex", [128, 4, GK], I32)
        corners = sb("corners", [128, 4, GK, CG])
        sampled = sb("sampled", [128, K, G, CG])
        samples_t = sb("samples_t", [C, K, W])
        u = sb("u", [C, W])
        z = sb("z", [C, W])
        turn_ps = psum("turn_ps", [128, 3, BANK])
        offs_ps = psum("offs_ps", [128, BANK])
        out_ps = psum("out_ps", [128, BANK])

        (loaded, ready, h_in, h_turned, h_copied, h_stored, row_in, row_free, conv_done, mask_ready, chain,
         index_ready, gathered, row_gathered, blended, turned, copied, contracted, ulin_ready, u_ready, c1_done,
         zlin_ready, row_stored) = (sem(n) for n in """loaded ready h_in h_turned h_copied h_stored row_in row_free
         conv_done mask_ready chain index_ready gathered row_gathered blended turned copied contracted ulin_ready
         u_ready c1_done zlin_ready row_stored""".split())
        sp_passed, pool_passed = sem("sp_passed"), sem("pool_passed")
        block = ctx.enter_context(nc.Block())

        def rows(engine, body):
            with engine.Fori(0, ROWS_ALL) as t:
                body(t, t // H, t % H)

        def where_large(engine):
            return engine.If(engine.value_load(is_large[0:1, 0:1], min_val=0, max_val=1) > 0)

        @block.sync
        def _(sp):
            with where_large(sp):
                for dst, src in ((ident, tables["ident"]), (wot, wo), (wdt, wd), (wct, wc), (taps, tables["taps"]),
                                 (xcol, tables["xcol"]), (bias_row, wo_bias.rearrange("p o -> o p"))):
                    sp.dma_start(dst[:], src).then_inc(loaded, 16)

                def turn(t, b, y):
                    sp.dma_start(hrow[:], hpad[b, :, y + 2, :]).then_inc(h_in, 16)
                    sp.wait_ge(h_copied, t + 1)
                    sp.dma_start(hpix[bass.ds(t * W, W), :], hrow_t[:]).then_inc(h_stored, 16)
                    sp.wait_ge(h_stored, 16 * (t + 1))
                    sp.sem_inc(sp_passed, 1)

                rows(sp, turn)
                sp.wait_ge(ready, 3)

                def body(t, b, y):
                    sp.wait_ge(row_free, t + 1)
                    sp.dma_start(rows_h[:, :, 1:W + 1], hpad[b, :, bass.ds(y + 1, KS), :]).then_inc(row_in, 16)
                    sp.dma_start(xrow[:], xpad[b, :, y + 1, :]).then_inc(row_in, 16)
                    sp.dma_start(rowpos[:], tables["rowpos"][t]).then_inc(row_in, 16)
                    sp.wait_ge(row_free, t + 2)
                    sp.dma_start(out[b, :, y, :], z[:]).then_inc(row_stored, 16)
                    sp.wait_ge(row_stored, 16 * (t + 1))
                    sp.sem_inc(sp_passed, 1)

                rows(sp, body)

        @block.gpsimd
        def _(pool):
            with where_large(pool):
                nc.gpsimd.memset(ones[:], 1.0).then_inc(ready, 1)
                nc.gpsimd.memset(rows_h[:], 0.0).then_inc(ready, 1)
                pool.wait_ge(ready, 2)
                nc.gpsimd.memset(u[:], 0.0).then_inc(ready, 1)
                pool.wait_ge(ready, 3)
                nc.gpsimd.memset(z[:], 0.0).then_inc(row_free, 1)
                pool.wait_ge(h_stored, 16 * ROWS_ALL)
                table = hpix.rearrange("n (g c) -> (n g) c", g=G)

                def body(t, b, y):
                    pool.wait_ge(index_ready, t + 1)
                    pool.sem_inc(pool_passed, 1)
                    for n in range(4 * GK):
                        pool.indirect_dma_start(
                            out=corners[:].rearrange("p a c e -> p (a c) e")[:, n, :], out_offset=None, in_=table,
                            in_offset=bass.IndirectOffsetOnAxis(
                                ap=cindex[:].rearrange("p a c -> p (a c)")[:, n:n + 1], axis=0)
                        ).then_inc(gathered, 16)
                    pool.wait_ge(gathered, 16 * 4 * GK)
                    pool.dma_reset()
                    pool.sem_clear(gathered)
                    pool.sem_inc(row_gathered, 1)

                rows(pool, body)

        @block.tensor
        def _(pe):
            with where_large(pe):
                pe.wait_ge(loaded, 16 * 7)
                pe.wait_ge(ready, 3)

                def turn(t, b, y):
                    pe.wait_ge(h_in, 16 * (t + 1))
                    nc.tensor.transpose(turn_ps[:, 0, 0:C], hrow[:], ident[:]).then_inc(h_turned, 1)

                rows(pe, turn)

                def body(t, b, y):
                    pe.wait_ge(row_in, 48 * (t + 1))
                    for k in range(K):
                        nc.tensor.matmul(offs_ps[:, 0:NV], rows_h[:, k // KS, k % KS:k % KS + W], wot[:, k, 0:NV],
                                         start=(k == 0), stop=False)
                    nc.tensor.matmul(offs_ps[:, 0:NV], ones[:], bias_row[:, 0:NV], start=False, stop=True
                                     ).then_inc(conv_done, 1)
                    pe.wait_ge(blended, t + 1)
                    for k in range(K):
                        mm = nc.tensor.transpose(turn_ps[:, k // 4, (k % 4) * C:(k % 4) * C + C],
                                                 sampled[:, k].rearrange("p g c -> p (g c)"), ident[:])
                    mm.then_inc(turned, 1)
                    pe.wait_ge(copied, t + 1)
                    for k in range(K):
                        mm = nc.tensor.matmul(out_ps[:, 0:W], wdt[:, k, :], samples_t[:, k, :], start=(k == 0),
                                              stop=(k == K - 1))
                    mm.then_inc(contracted, 1)
                    pe.wait_ge(u_ready, t + 1)
                    nc.tensor.matmul(out_ps[:, 0:W], wct[:], u[:], start=True, stop=True).then_inc(c1_done, 1)

                rows(pe, body)

        @block.scalar
        def _(act):
            with where_large(act):
                def turn(t, b, y):
                    act.wait_ge(h_turned, t + 1)
                    nc.scalar.copy(hrow_t[:], turn_ps[:, 0, 0:C]).then_inc(h_copied, 1)

                rows(act, turn)

                def body(t, b, y):
                    act.wait_ge(conv_done, t + 1)
                    nc.scalar.activation(mask[:], offs_ps[:, V_M:V_M + GK], ACT.Sigmoid).then_inc(mask_ready, 1)
                    act.wait_ge(turned, t + 1)
                    flat = samples_t[:].rearrange("c k w -> c (k w)")
                    for r in range(3):
                        m = min(BANK, K * W - BANK * r)
                        last = nc.scalar.copy(flat[:, BANK * r:BANK * r + m], turn_ps[:, r, 0:m])
                    last.then_inc(copied, 1)
                    act.wait_ge(contracted, t + 1)
                    nc.scalar.activation(u[:], out_ps[:, 0:W], ACT.Identity, bias=bn[:, 6:7], scale=bn[:, 2:3]
                                         ).then_inc(ulin_ready, 1)
                    act.wait_ge(c1_done, t + 1)
                    nc.scalar.activation(z[:], out_ps[:, 0:W], ACT.Identity, bias=bn[:, 7:8], scale=bn[:, 3:4]
                                         ).then_inc(zlin_ready, 1)

                rows(act, body)

        @block.vector
        def _(dve):
            V = nc.vector
            STEPS = 42

            def body(t, b, y):
                n = [0]

                def link(instruction):
                    n[0] += 1
                    instruction.then_inc(chain, 1)
                    dve.wait_ge(chain, STEPS * t + n[0])

                dve.wait_ge(conv_done, t + 1)
                dve.wait_ge(row_in, 48 * (t + 1))
                dve.wait_ge(mask_ready, t + 1)
                axes = ((V_OY, rowpos[:, 0:1], H), (V_OX, xcol[:, 0:1], W))
                for a, (col, position, size) in enumerate(axes):
                    link(V.scalar_tensor_tensor(coord[:, a], offs_ps[:, col:col + GK], position, taps[:, a], ALU.add,
                                                ALU.add))
                    link(V.tensor_scalar(coord[:, a], coord[:, a], -2.0, float(size), ALU.max, ALU.min))
                link(V.tensor_copy(whole[:], coord[:]))
                link(V.tensor_copy(low[:], whole[:]))
                link(V.tensor_tensor(work[:], low[:], coord[:], ALU.is_gt))
                link(V.tensor_tensor(low[:], low[:], work[:], ALU.subtract))
                link(V.tensor_tensor(side[:, :, 1], coord[:], low[:], ALU.subtract))
                link(V.tensor_scalar(side[:, :, 0], side[:, :, 1], -1.0, 1.0, ALU.mult, ALU.add))
                link(V.tensor_copy(place[:, :, 0], low[:]))
                link(V.tensor_scalar(place[:, :, 1], low[:], 1.0, None, ALU.add))
                for a, (_, _, size) in enumerate(axes):
                    for corner in range(2):
                        p, s = place[:, a, corner], side[:, a, corner]
                        link(V.tensor_scalar(work[:, 0], p, 0.0, None, ALU.is_ge))
                        link(V.tensor_tensor(s, s, work[:, 0], ALU.mult))
                        link(V.tensor_scalar(work[:, 0], p, float(size - 1), None, ALU.is_le))
                        link(V.tensor_tensor(s, s, work[:, 0], ALU.mult))
                        link(V.tensor_scalar(p, p, 0.0, float(size - 1), ALU.max, ALU.min))
                for corner in range(2):
                    p = place[:, 0, corner]
                    link(V.tensor_scalar(p, p, float(W * G), rowpos[:, 1:2], ALU.mult, ALU.add))
                    q = place[:, 1, corner]
                    link(V.scalar_tensor_tensor(q, q, float(G), taps[:, 2], ALU.mult, ALU.add))
                for i in range(4):
                    V.tensor_tensor(cindex_f[:, i], place[:, 0, i // 2], place[:, 1, i % 2], ALU.add)
                    last = V.tensor_tensor(cweight[:, i], side[:, 0, i // 2], side[:, 1, i % 2], ALU.mult)
                link(last)
                V.tensor_copy(cindex[:], cindex_f[:]).then_inc(index_ready, 1)
                link(V.tensor_tensor(cweight[:], cweight[:], mask[:].unsqueeze(1).to_broadcast([128, 4, GK]), ALU.mult))
                dve.wait_ge(row_gathered, t + 1)
                flat = corners[:].rearrange("p a c e -> p (a c) e")
                link(V.tensor_tensor(flat, flat, cweight[:].rearrange("p a c -> p (a c)").unsqueeze(2).to_broadcast(
                    [128, 4 * GK, CG]), ALU.mult))
                link(V.tensor_tensor(corners[:, 0], corners[:, 0], corners[:, 1], ALU.add))
                link(V.tensor_tensor(corners[:, 2], corners[:, 2], corners[:, 3], ALU.add))
                V.tensor_tensor(sampled[:].rearrange("p k g e -> p g k e"),
                                corners[:, 0].rearrange("p (g k) e -> p g k e", g=G),
                                corners[:, 2].rearrange("p (g k) e -> p g k e", g=G), ALU.add).then_inc(blended, 1)
                dve.wait_ge(ulin_ready, t + 1)
                V.scalar_tensor_tensor(u[:], u[:], SLOPE, u[:], ALU.mult, ALU.max).then_inc(u_ready, 1)
                dve.wait_ge(zlin_ready, t + 1)
                link(V.scalar_tensor_tensor(z[:], z[:], SLOPE, z[:], ALU.mult, ALU.max))
                assert n[0] == STEPS, n[0]
                V.tensor_tensor(z[:], z[:], xrow[:], ALU.add).then_inc(row_free, 1)

            with where_large(dve):
                dve.wait_ge(loaded, 16 * 7)
                rows(dve, body)


def build(nc, shape, d):
    B, _, H, W = shape
    h1pad = nc.dram_tensor("h1pad", [B, C, H + 2, W], F32).ap()
    hpad = nc.dram_tensor("hpad", [B, C, H + 4, W], F32).ap()
    offsets = nc.dram_tensor("offsets", [B, NV, H, W], F32).ap()
    hpix = nc.dram_tensor("hpix", [B * H * W, C], F32).ap()
    with nc.sbuf_tensor("is_large", [1, 1], I32) as is_large, nc.sbuf_tensor("chan", [C, 20], F32) as chan, nc.sbuf_tensor("bn", [C, 9], F32) as bn, \
            nc.sbuf_tensor("work", [C, 16], F32) as work:
        convolution_block(nc, B, H, W, d["xpad"], d["chan"], d["w1"], d["w2"], d["wo"], d["wo_bias"], h1pad, hpad,
                          offsets, chan, bn, work)
        deformable_block(nc, B, H, W, d["xpad"], hpad, offsets, d["out"], d, d["wd"], d["wc"], bn, is_large)
        general_block(nc, B, H, W, d["xpad"], hpad, hpix, d["out"], d, d["wo"], d["wo_bias"], d["wd"], d["wc"], bn, is_large)


def lay_out(x, rb_w1, rb_b1, rb_bn1, rb_w2, rb_b2, rb_bn2, off_w, off_b, dc_w, dc_b, bn1, cv2_w, bn2):
    B, _, H, W = x.shape
    xpad = np.zeros((B, C, H + 2, W), np.float32)
    xpad[:, :, 1:H + 1] = x

    def taps(w):
        return np.ascontiguousarray(w.reshape(w.shape[0], C, -1).transpose(1, 2, 0))

    ow = taps(off_w)
    wo = np.zeros((C, K, HALF_V), np.float32)
    wo_bias = np.zeros((128, 1), np.float32)
    n = 2 * GK
    for row, src in ((V_OY, slice(0, n, 2)), (V_M, slice(n, n + GK)), (V_OX, slice(1, n, 2))):
        wo[:, :, row:row + GK] = ow[:, :, src]
        for half in (0, HALF_V):
            wo_bias[half + row:half + row + GK, 0] = off_b[src]
    bns = (rb_bn1, rb_bn2, bn1, bn2)
    chan = np.stack([bn[i] for i in range(4) for bn in bns] + [rb_b1, rb_b2, dc_b, np.zeros(C, np.float32)], 1)
    return dict(xpad=xpad, chan=np.ascontiguousarray(chan), w1=taps(rb_w1), w2=taps(rb_w2), wo=wo, wo_bias=wo_bias,
                wd=taps(dc_w), wc=np.ascontiguousarray(taps(cv2_w)[:, 0]), **constants(B, H, W))


def kernel(**inputs):
    import concourse.bacc as bacc
    from concourse.bass_utils import run_bass_kernel_spmd

    inputs = {name.replace("L0_conv_", ""): np.asarray(a) for name, a in inputs.items()}
    arrays = lay_out(**inputs)
    shape = inputs["x"].shape
    nc = bacc.Bacc("TRN2", target_bir_lowering=False, num_devices=1)
    d = {name: nc.dram_tensor(f"in_{name}", a.shape, mybir.dt.from_np(a.dtype), kind="ExternalInput").ap()
         for name, a in arrays.items()}
    d["out"] = nc.dram_tensor("out", shape, F32, kind="ExternalOutput").ap()
    build(nc, shape, d)
    result = run_bass_kernel_spmd(nc, [{f"in_{name}": a for name, a in arrays.items()}], core_ids=[0])
    return result.results[0]["out"]
```

```python
from contextlib import ExitStack

import numpy as np

import concourse.bass as bass
from concourse import mybir

ALU = mybir.AluOpType
ACT = mybir.ActivationFunctionType
AX = mybir.AxisListType
F32 = mybir.dt.float32
F32R = mybir.dt.float32r
F16 = mybir.dt.float16
I32 = mybir.dt.int32

C = 128
G = 2
CG = C // G
KS = 3
K = KS * KS
GK = G * K
EPS = 1e-5
SLOPE = 0.1
BANK = 512
MSCALE = 32768.0

ROWS = 4
PX = 12
QY, QX = ROWS + 4, PX + 4
assert QY * QX == 128
V_OY, V_M, V_OX = 0, GK, 2 * GK
NV = 3 * GK
HALF_V = 64
X_ROW = 64
DISP = (0, -1, 1)
NHAT = len(DISP)
YROWS = 2 * NHAT * GK
CROWS = 16


def pixel_columns(W):
    return -(-W // PX) * PX + QX - PX


def constants(B, H, W):
    q = np.arange(128)
    qy, qx = q // QX, q % QX
    selx = np.zeros((128, GK, 128), np.float16)
    for g in range(G):
        for k in range(K):
            c = g * K + k
            selx[X_ROW + c, c] = 1
            selx[X_ROW + GK + c, c] = 1
            selx[0, c] = 1
            selx[1, c] = (k % KS) - 1 + 2 - qx
    sely = np.zeros((YROWS, GK, ROWS - 1 + QY, QX), np.float16)
    for c in range(GK):
        for d in range(NHAT):
            for part in range(2):
                sely[(part * NHAT + d) * GK + c, c, ROWS - 1 + 2 + (c % K) // KS - 1 + DISP[d]] = 1
    xpos = np.zeros((2, ROWS, W), np.float16)
    xpos[0] = np.arange(W) % PX
    xpos[1] = 1
    cols = np.zeros((128, 4), np.float32)
    for part in range(2):
        for d in range(NHAT):
            rows = slice((part * NHAT + d) * GK, (part * NHAT + d + 1) * GK)
            cols[rows, 0] = -DISP[d]
            cols[rows, 1] = -part
    cols[X_ROW + GK:X_ROW + 2 * GK, 2] = -1
    cols[0:GK, 3] = 1
    cols[X_ROW:X_ROW + 2 * GK, 3] = 1
    ch = np.arange(GK)
    taps = np.zeros((128, 3, GK), np.float32)
    taps[:, 0] = (ch % K) // KS - 1
    taps[:, 1] = (ch % K) % KS - 1
    taps[:, 2] = ch // K
    xcol = np.arange(128, dtype=np.float32)[:, None]
    rowpos = np.zeros((B * H, 128, 2), np.float32)
    rowpos[:, :, 0] = (np.arange(B * H) % H)[:, None]
    WP = pixel_columns(W)
    rowpos[:, :, 1] = ((np.arange(B * H) // H * (H + 4) + 2) * WP * G + 2 * G)[:, None]
    return dict(taps=taps, xcol=xcol, rowpos=rowpos, selx=selx, sely=sely, xpos=xpos, cols=cols,
                ident=np.eye(128, dtype=np.float32))




def at_least(engine, sem, value):
    if isinstance(value, int) and value <= 0:
        return
    engine.wait_ge(sem, value)


def batch_norm_columns(nc, chan, bn, work, sems):
    chan_loaded, bn_sqrt, bn_step, bn_ready = sems
    gamma, beta, mean, var, cbias = (chan[:, 4 * i:4 * i + 4] for i in range(5))
    a, s, r, t = (work[:, 4 * i:4 * i + 4] for i in range(4))

    def act_part(act):
        act.wait_ge(bn_step, 1)
        nc.scalar.activation(s, a, ACT.Sqrt).then_inc(bn_sqrt, 1)

    def dve_part(dve):
        n = [0]

        def step(instruction):
            n[0] += 1
            instruction.then_inc(bn_step, 1)
            dve.wait_ge(bn_step, n[0])

        dve.wait_ge(chan_loaded, 48)
        step(nc.vector.tensor_scalar(a, var, EPS, None, ALU.add))
        dve.wait_ge(bn_sqrt, 1)
        step(nc.vector.reciprocal(r, s))
        for _ in range(2):
            step(nc.vector.tensor_tensor(t, r, r, ALU.mult))
            step(nc.vector.tensor_tensor(t, t, a, ALU.mult))
            step(nc.vector.tensor_scalar(t, t, -0.5, 1.5, ALU.mult, ALU.add))
            step(nc.vector.tensor_tensor(r, r, t, ALU.mult))
        step(nc.vector.tensor_tensor(bn[:, 0:4], gamma, r, ALU.mult))
        step(nc.vector.tensor_tensor(t, mean, bn[:, 0:4], ALU.mult))
        step(nc.vector.tensor_tensor(s, cbias, bn[:, 0:4], ALU.mult))
        step(nc.vector.tensor_tensor(t, beta, t, ALU.subtract))
        step(nc.vector.tensor_tensor(bn[:, 4:8], t, s, ALU.add))
        step(nc.vector.tensor_scalar(bn[:, 8:9], bn[:, 2:3], 1.0 / MSCALE, None, ALU.mult))
        nc.vector.tensor_copy(work[:, 15:16], bn[:, 8:9]).then_inc(bn_ready, 1)

    return act_part, dve_part


def convolution_block(nc, B, H, W, xpad, chan_d, w1, w2, w3, w3_bias, h1pad, hpad, hpix, offsets, ident_d, chan, bn,
                      work):
    PER = H // CROWS
    NS = B * PER
    TURNS = NS // 2
    PAIRS = W // 2
    WP = pixel_columns(W)
    M = 4
    HALVES = 2
    HR = CROWS // HALVES
    ORDER = (2, 1, 0, 3)
    CONV1, CONV2, CONV3 = range(3)
    inputs, outputs = (xpad, h1pad, hpad), (h1pad, hpad, offsets)
    first_row = (0, 0, 1)
    out_row = (1, 2, 0)
    assert HR * PAIRS == BANK and B > 1 and 2 * HALF_V == C
    with ExitStack() as ctx:
        def sb(name, shape, dt=F32):
            return ctx.enter_context(nc.sbuf_tensor(name, shape, dt))

        def sem(name):
            return ctx.enter_context(nc.semaphore(name))

        w_raw = sb("w_raw", [C, KS, KS, C])
        w_ends = sb("w_ends", [C, KS, C])
        w_mixed = sb("w_mixed", [C, KS, M, C])
        w_hi = [sb(f"w_hi{c}", [C, KS, M, C], F32R) for c in range(2)]
        w_lo = [sb(f"w_lo{c}", [C, KS, M, C], F32R) for c in range(2)]
        bias3 = sb("bias3", [C, 1])
        ident = sb("ident3", [128, 128])
        rows_in = [sb(f"rows_in{p}", [C, CROWS + 2, W + 2]) for p in range(2)]
        exact = sb("exact", [C, M, CROWS + 2, PAIRS])
        in_hi = [sb(f"in_hi{p}", [C, M, CROWS + 2, PAIRS], F32R) for p in range(2)]
        in_lo = [sb(f"in_lo{p}", [C, M, CROWS + 2, PAIRS], F32R) for p in range(2)]
        x_res = [sb(f"x_res{p}", [C, HALVES, HR * W]) for p in range(2)]
        m2 = [sb(f"m2_{h}", [C, BANK]) for h in range(HALVES)]
        middle = sb("middle", [C, 2, BANK])
        summed = [sb(f"summed{h}", [C, HR * PAIRS, 2]) for h in range(HALVES)]
        rows_out = [sb(f"rows_out{h}", [C, HR * W]) for h in range(HALVES)]
        pixels = x_res
        zeros = sb("zeros", [C, 2 * WP * C // 128])
        acc = [ctx.enter_context(nc.psum_tensor(f"acc{h}", [C, M, BANK], F32)) for h in range(HALVES)]

        chan_loaded, bn_sqrt, bn_step, bn_ready = (sem(n) for n in ("chan_loaded", "bn_sqrt", "bn_step", "bn_ready"))
        w_loaded, w_ends_ready, w_mixed_ready = sem("w_loaded"), sem("w_ends_ready"), sem("w_mixed_ready")
        w_hi_ready, w_lo_ready = sem("w_hi_ready"), sem("w_lo_ready")
        zeros_ready, zeros_stored, borders_zero = sem("zeros_ready"), sem("zeros_stored"), sem("borders_zero")
        rows_loaded = [sem(f"rows_loaded{p}") for p in range(2)]
        res_loaded = [sem(f"res_loaded{p}") for p in range(2)]
        transformed, hi_ready, lo_ready = sem("transformed"), sem("hi_ready"), sem("lo_ready")
        product_done, m2_ready, middle_ready, pair_ready = (
            sem(n) for n in ("product_done", "m2_ready", "middle_ready", "pair_ready"))
        sum_done, out_ready = sem("sum_done"), sem("out_ready")
        out_stored = [sem(f"out_stored{h}") for h in range(HALVES)]
        rows_turned, pixels_ready = sem("rows_turned"), sem("pixels_ready")
        pixels_stored = [sem(f"pixels_stored{p}") for p in range(2)]
        sp_passed, pool_passed = sem("sp_passed"), sem("pool_passed")
        bn_act, bn_dve = batch_norm_columns(nc, chan, bn, work, (chan_loaded, bn_sqrt, bn_step, bn_ready))
        block = ctx.enter_context(nc.Block())

        def fills_before(conv, s):
            if isinstance(s, int) and s < 0 and conv > 0:
                conv, s = conv - 1, s + NS
            return HALVES * (NS * conv + s) if conv < CONV3 else HALVES * NS * CONV3 + s

        def fills(conv):
            return HALVES if conv < CONV3 else 1

        def strips(engine, body):
            for conv in range(3):
                def turn(i):
                    for p in range(2):
                        body(conv, 2 * i + p, p)

                turn(0)
                if TURNS > 2:
                    with engine.Fori(1, TURNS - 1) as i:
                        turn(i)
                turn(TURNS - 1)

        def two_ahead(engine, prepare, results, norms):
            def body(conv, s, p):
                def ahead():
                    if isinstance(s, int) and s + 2 >= NS:
                        if conv + 1 < CONV3:
                            prepare(conv + 1, s + 2 - NS, p)
                    elif conv < CONV3:
                        prepare(conv, s + 2, p)

                results(conv, s, p, ahead)

            prepare(CONV1, 0, 0)
            norms()
            prepare(CONV1, 1, 1)
            strips(engine, body)

        @block.sync
        def _(sp):
            sp.dma_start(w_raw[:].rearrange("c y x o -> c (y x) o"), w1).then_inc(w_loaded, 16)

            def store_zeros():
                sp.wait_ge(zeros_ready, 1)
                for b in range(B):
                    for y in (0, H + 1):
                        sp.dma_start(h1pad[b, :, y, :], zeros[:, 0:W]).then_inc(zeros_stored, 16)
                    for y in (0, H + 2):
                        sp.dma_start(hpad[b, :, y:y + 2, :], zeros[:, 0:2 * W].rearrange("c (r w) -> c r w", w=W)
                                      ).then_inc(zeros_stored, 16)
                        sp.dma_start(hpix[b, y:y + 2].rearrange("y x c -> (y x c)").rearrange("(p f) -> p f", p=128),
                                      zeros[:]).then_inc(zeros_stored, 16)
                    for x in range(0, WP - W, 2):
                        x += W if x else 0
                        sp.dma_start(hpix[b, 2:H + 2, x:x + 2, :].rearrange("y x c -> y (x c)"), zeros[0:H, 0:2 * C]
                                      ).then_inc(zeros_stored, 16)

            def load(conv, s, p):
                b, y = s // PER, (s % PER) * CROWS
                if isinstance(s, int) and s == 0 and conv > 0:
                    sp.wait_ge(zeros_stored, 16 * 10 * B)
                if conv > 0:
                    for h in range(HALVES):
                        sp.wait_ge(out_stored[h], (conv - 1) * 16 * NS + (b + 1) * (16 * PER))
                        sp.sem_inc(sp_passed, 1)
                at_least(sp, transformed, M * (NS * conv + s - 1))
                sp.sem_inc(sp_passed, 1)
                if conv == CONV3:
                    at_least(sp, rows_turned, HALVES * (s - 1))
                    sp.sem_inc(sp_passed, 1)
                sp.dma_start(rows_in[p][:, :, 1:W + 1], inputs[conv][b, :, bass.ds(y + first_row[conv], CROWS + 2), :]
                             ).then_inc(rows_loaded[p], 16)
                if conv == CONV2:
                    at_least(sp, sum_done, HALVES * (s - 1))
                    sp.sem_inc(sp_passed, 1)
                    sp.dma_start(x_res[p][:].rearrange("c h (r w) -> c (h r) w", w=W),
                                 xpad[b, :, bass.ds(y + 1, CROWS), :]).then_inc(res_loaded[p], 16)
                if isinstance(s, int) and s == 1 and conv == CONV1:
                    store_zeros()
                if isinstance(s, int) and s == 1 and conv < CONV3:
                    sp.wait_ge(w_mixed_ready, M * (conv + 1))
                    if conv == CONV1:
                        sp.dma_start(w_raw[:].rearrange("c y x o -> c (y x) o"), w2).then_inc(w_loaded, 16)
                    else:
                        sp.dma_start(w_raw[:, :, :, 0:HALF_V].rearrange("c y x o -> c (y x) o"), w3
                                     ).then_inc(w_loaded, 16)

            strips(sp, load)
            for h in range(HALVES):
                sp.wait_ge(out_stored[h], 16 * 2 * NS + 32 * TURNS)
                sp.wait_ge(pixels_stored[h], 16 * TURNS)

        @block.gpsimd
        def _(pool):
            for p in range(2):
                for x in (0, W + 1):
                    nc.gpsimd.memset(rows_in[p][:, :, x:x + 1], 0.0).then_inc(borders_zero, 1)
            nc.gpsimd.memset(zeros[:], 0.0).then_inc(zeros_ready, 1)
            pool.wait_ge(borders_zero, 4)

            def transform(conv, s, p):
                n = NS * conv + s
                pairs = rows_in[p][:].rearrange("c r (i e) -> c r i e", e=2)
                d = [pairs[:, :, e // 2:e // 2 + PAIRS, e % 2] for e in range(4)]
                pool.wait_ge(rows_loaded[p], 16 * (s // 2 + 1 + TURNS * conv))
                for k, m in enumerate(ORDER):
                    if conv == CONV3 and not (isinstance(s, int) and s == 0):
                        pool.wait_ge(product_done, M * (fills_before(conv, s) - 1) + k + 1)
                    else:
                        at_least(pool, lo_ready, M * (n - 1) + k + 1)
                    pool.sem_inc(pool_passed, 1)
                    first, second, op = ((d[0], d[2], ALU.subtract), (d[1], d[2], ALU.add),
                                         (d[2], d[1], ALU.subtract), (d[1], d[3], ALU.subtract))[m]
                    nc.gpsimd.tensor_tensor(exact[:, m], first, second, op).then_inc(transformed, 1)

            strips(pool, transform)

        @block.tensor
        def _(pe):
            def convolve(conv, s, p):
                if isinstance(s, int) and s == 0:
                    pe.wait_ge(w_lo_ready, conv + 1)
                for h in range(HALVES):
                    at_least(pe, pair_ready, 2 * (fills_before(conv, s) + h - 1))
                    for k, m in enumerate(ORDER):
                        if h == 0:
                            pe.wait_ge(lo_ready, M * (NS * conv + s) + k + 1)
                        for dy in range(KS):
                            y = HR * h + dy
                            for part, (w, rows) in enumerate(((w_hi, in_hi), (w_hi, in_lo), (w_lo, in_hi))):
                                mm = nc.tensor.matmul(acc[h][:, m, :], w[conv][:, dy, m, :], rows[p][:, m, y:y + HR, :],
                                                      start=(dy == 0 and part == 0), stop=(dy == KS - 1 and part == 2))
                        mm.then_inc(product_done, 1)

            def convolve_h(s, p):
                if isinstance(s, int) and s == 0:
                    pe.wait_ge(w_mixed_ready, M * (CONV3 + 1))
                n = fills_before(CONV3, s)
                for k, m in enumerate(ORDER):
                    pe.wait_ge(transformed, M * (NS * CONV3 + s) + k + 1)
                    pe.wait_ge(*((m2_ready, n), (middle_ready, 2 * n), (pair_ready, 2 * n - 1), (pair_ready, 2 * n))[k])
                    for dy in range(KS):
                        for h in range(HALVES):
                            y = HR * h + dy
                            mm = nc.tensor.matmul(acc[0][HALF_V * h:HALF_V * h + HALF_V, m, :],
                                                  w_mixed[:, dy, m, 0:HALF_V], exact[:, m, y:y + HR, :],
                                                  start=(dy == 0), stop=(dy == KS - 1))
                    mm.then_inc(product_done, 1)
                at_least(pe, pixels_ready, HALVES * s)
                for r in range(CROWS):
                    mm = nc.tensor.transpose(acc[1][0:W, r // 4, r % 4 * C:r % 4 * C + C],
                                             rows_in[p][:, 1 + r, 1:W + 1], ident[:])
                    if (r + 1) % HR == 0:
                        mm.then_inc(rows_turned, 1)

            strips(pe, lambda conv, s, p: convolve(conv, s, p) if conv < CONV3 else convolve_h(s, p))

        @block.scalar
        def _(act):
            act.dma_start(chan[:], chan_d).then_inc(chan_loaded, 16)
            act.dma_start(bias3[:], w3_bias).then_inc(chan_loaded, 16)
            act.dma_start(ident[:], ident_d).then_inc(chan_loaded, 16)
            def round_rows(conv, s, p):
                n = NS * conv + s
                for k, m in enumerate(ORDER):
                    act.wait_ge(transformed, M * n + k + 1)
                    if k == 0:
                        at_least(act, product_done, M * fills_before(conv, s - 1))
                    nc.scalar.copy(in_hi[p][:, m], exact[:, m]).then_inc(hi_ready, 1)

            def keep_m2(conv, s, p, f):
                h = f if conv < CONV3 else p
                n = fills_before(conv, s) + f
                act.wait_ge(product_done, M * n + 1)
                at_least(act, middle_ready, 2 * (n - 1))
                nc.scalar.copy(m2[h][:], acc[h if conv < CONV3 else 0][:, 2, :]).then_inc(m2_ready, 1)

            def store(conv, s, p, f):
                b, y = s // PER, (s % PER) * CROWS
                h = f if conv < CONV3 else p
                n = fills_before(conv, s) + f
                if conv < CONV3:
                    at_least(act, out_stored[h], 16 * (NS * conv + s))
                else:
                    act.wait_ge(out_stored[h], 16 * 2 * NS + 32 * (s // 2))
                pairs = summed[h][:].rearrange("c i e -> c (i e)")
                if conv == CONV1:
                    act.wait_ge(pair_ready, 2 * (n + 1))
                    nc.scalar.activation(rows_out[h][:], pairs, ACT.Relu, bias=bn[:, 4:5], scale=bn[:, 0:1]
                                         ).then_inc(out_ready, 1)
                elif conv == CONV2:
                    act.wait_ge(sum_done, HALVES * s + f + 1)
                    nc.scalar.activation(rows_out[h][:], pairs, ACT.Relu, bias=bn[:, 5:6]).then_inc(out_ready, 1)
                else:
                    act.wait_ge(pair_ready, 2 * (n + 1))
                    nc.scalar.activation(rows_out[h][:], pairs, ACT.Identity, bias=bias3[:]).then_inc(out_ready, 1)
                act.wait_ge(out_ready, n + 1)
                rows = rows_out[h][:].rearrange("c (r w) -> c r w", w=W)
                if conv < CONV3:
                    act.dma_start(outputs[conv][b, :, bass.ds(y + out_row[conv] + HR * f, HR), :], rows
                                  ).then_inc(out_stored[h], 16)
                else:
                    for z in range(HALVES):
                        act.dma_start(offsets[b, :, bass.ds(y + HR * z, HR), :], rows[HALF_V * z:HALF_V * z + NV]
                                      ).then_inc(out_stored[h], 16)

            def norms():
                bn_act(act)
                act.wait_ge(bn_ready, 1)

            def results(conv, s, p, ahead):
                for f in range(fills(conv)):
                    keep_m2(conv, s, p, f)
                for f in range(fills(conv)):
                    if f == fills(conv) - 1:
                        ahead()
                    store(conv, s, p, f)
                if conv == CONV3:
                    b, y = s // PER, (s % PER) * CROWS
                    act.wait_ge(rows_turned, HALVES * s + 1)
                    if isinstance(s, int) and s < 2:
                        act.wait_ge(sum_done, HALVES * NS)
                    else:
                        act.wait_ge(pixels_stored[p], 16 * (s // 2))
                    nc.scalar.copy(pixels[p][0:W, 0, :], acc[1][0:W, 0:2, :].rearrange("x a b -> x (a b)")
                                   ).then_inc(pixels_ready, 1)
                    act.wait_ge(pixels_ready, HALVES * (s + 1))
                    act.dma_start(hpix[b, bass.ds(y + 2, CROWS), 2:W + 2, :].rearrange("y x c -> x y c"),
                                  pixels[p][0:W].rearrange("x h (y c) -> x (h y) c", c=C)
                                  ).then_inc(pixels_stored[p], 16)

            two_ahead(act, round_rows, results, norms)

        @block.vector
        def _(dve):
            def mix_weights(conv):
                n = C if conv < CONV3 else HALF_V
                g = [w_raw[:, :, x, 0:n] for x in range(KS)]
                ends, mixed = w_ends[:, :, 0:n], w_mixed[:, :, :, 0:n]
                dve.wait_ge(w_loaded, 16 * (conv + 1))
                at_least(dve, w_lo_ready, conv)
                nc.vector.tensor_tensor(ends, g[0], g[2], ALU.add).then_inc(w_ends_ready, 1)
                dve.wait_ge(w_ends_ready, 2 * conv + 1)
                nc.vector.tensor_scalar(ends, ends, 0.5, None, ALU.mult).then_inc(w_ends_ready, 1)
                dve.wait_ge(w_ends_ready, 2 * conv + 2)
                for m, sign in ((1, 0.5), (2, -0.5)):
                    nc.vector.scalar_tensor_tensor(mixed[:, :, m, :], g[1], sign, ends, ALU.mult, ALU.add
                                                   ).then_inc(w_mixed_ready, 1)
                for m, x in ((0, 0), (3, 2)):
                    nc.vector.tensor_copy(mixed[:, :, m, :], g[x]).then_inc(w_mixed_ready, 1)
                dve.wait_ge(w_mixed_ready, M * (conv + 1))
                if conv < CONV3:
                    nc.vector.tensor_copy(w_hi[conv][:], mixed).then_inc(w_hi_ready, 1)
                    dve.wait_ge(w_hi_ready, conv + 1)
                    nc.vector.tensor_tensor(w_lo[conv][:], mixed, w_hi[conv][:].bitcast(F32), ALU.subtract
                                            ).then_inc(w_lo_ready, 1)

            def split_rows(conv, s, p):
                n = NS * conv + s
                for k, m in enumerate(ORDER):
                    dve.wait_ge(hi_ready, M * n + k + 1)
                    nc.vector.tensor_tensor(in_lo[p][:, m], exact[:, m], in_hi[p][:, m].bitcast(F32),
                                            ALU.subtract).then_inc(lo_ready, 1)

            def combine(conv, s, p, ahead):
                for f in range(fills(conv)):
                    h = f if conv < CONV3 else p
                    a = acc[h if conv < CONV3 else 0]
                    n = fills_before(conv, s) + f
                    dve.wait_ge(m2_ready, n + 1)
                    dve.wait_ge(product_done, M * n + 2)
                    at_least(dve, pair_ready, 2 * n)
                    for e, op in enumerate((ALU.add, ALU.subtract)):
                        nc.vector.tensor_tensor(middle[:, e, :], a[:, 1, :], m2[h][:], op
                                                ).then_inc(middle_ready, 1)
                    dve.wait_ge(middle_ready, 2 * n + 1)
                    dve.wait_ge(product_done, M * n + 3)
                    at_least(dve, out_ready, n - 1)
                    nc.vector.tensor_tensor(summed[h][:, :, 0], a[:, 0, :], middle[:, 0, :], ALU.add
                                            ).then_inc(pair_ready, 1)
                    dve.wait_ge(middle_ready, 2 * n + 2)
                    dve.wait_ge(product_done, M * n + 4)
                    nc.vector.tensor_tensor(summed[h][:, :, 1], middle[:, 1, :], a[:, 3, :], ALU.subtract
                                            ).then_inc(pair_ready, 1)
                    if conv == CONV2:
                        pairs = summed[h][:].rearrange("c i e -> c (i e)")
                        dve.wait_ge(pair_ready, 2 * (n + 1))
                        dve.wait_ge(res_loaded[p], 16 * (s // 2 + 1))
                        nc.vector.scalar_tensor_tensor(pairs, pairs, bn[:, 1:2], x_res[p][:, h, :], ALU.mult, ALU.add
                                                       ).then_inc(sum_done, 1)
                ahead()
                if isinstance(s, int) and s == 1 and conv < CONV3:
                    mix_weights(conv + 1)
                if conv == CONV3:
                    dve.wait_ge(rows_turned, HALVES * (s + 1))
                    if not (isinstance(s, int) and s < 2):
                        dve.wait_ge(pixels_stored[p], 16 * (s // 2))
                    nc.vector.tensor_copy(pixels[p][0:W, 1, :], acc[1][0:W, 2:4, :].rearrange("x a b -> x (a b)")
                                          ).then_inc(pixels_ready, 1)

            mix_weights(CONV1)

            def norms():
                bn_dve(dve)
                dve.wait_ge(bn_ready, 1)

            two_ahead(dve, split_rows, combine, norms)


def deformable_block(nc, B, H, W, xpad, hpix, offsets, out, tables, wd, wc, bn, is_large):
    PER = H // ROWS
    NS = B * PER
    N = ROWS * W
    assert N == BANK
    NP = -(-W // PX)
    width = [min(PX, W - PX * i) for i in range(NP)]
    PSTEP = [range(max(2 * j - 1, 0), min(2 * j + 1, NP)) for j in range(K)]
    OSTEP = {6: range(0, 3), 7: range(3, 6), 8: range(6, 9)}
    assert max(j for j in range(K) if PSTEP[j]) < min(OSTEP)
    V_LOADS = 16 * 3
    with ExitStack() as ctx:
        def sb(name, shape, dt=F32):
            return ctx.enter_context(nc.sbuf_tensor(name, shape, dt))

        def sem(name):
            return ctx.enter_context(nc.semaphore(name))

        def psum(name, shape):
            return ctx.enter_context(nc.psum_tensor(name, shape, F32))

        selx = sb("selx", [128, GK, 128], F16)
        sely = sb("sely", [YROWS, GK, (ROWS - 1 + QY) * QX], F16)
        cols = sb("cols", [128, 4])
        wdt = sb("wdt", [C, K, C])
        wct = sb("wct", [C, C])
        patches = [sb(f"patches{p}", [128, NP, C]) for p in range(2)]
        vy = [sb(f"vy{p}", [YROWS, N]) for p in range(2)]
        vm = [sb(f"vm{p}", [YROWS, N]) for p in range(2)]
        vx = [sb(f"vx{p}", [128, N]) for p in range(2)]
        oabs = sb("oabs", [128, N])
        largest = sb("largest", [128, N])
        ox16 = sb("ox16", [128, N], F16)
        xrows = [sb(f"xrows{p}", [128, N], F16) for p in range(2)]
        yabs = sb("yabs", [YROWS, N])
        yhat = sb("yhat", [YROWS, N])
        mrep = sb("mrep", [YROWS, N])
        ywt = sb("ywt", [YROWS, N])
        ywt16 = sb("ywt16", [YROWS, N], F16)
        yrows = [sb(f"yrows{p}", [YROWS, N], F16) for p in range(2)]
        xabs = sb("xabs", [128, G, N])
        xhat = [sb(f"xhat{p}", [128, G, N]) for p in range(2)]
        A = [sb(f"A{p}", [128, K, G, N]) for p in range(2)]
        samples = sb("samples", [C, K, N])
        u = sb("u", [C, N])
        z = sb("z", [C, N])
        xres = [sb(f"xres{p}", [C, N]) for p in range(2)]
        vmax = sb("vmax", [128, 2])

        px = psum("px", [128, G, BANK])
        py = psum("py", [128, G, BANK])
        pg = [psum(f"pg{i}", [128, BANK]) for i in range(3)]
        po = psum("po", [128, BANK])

        names = """tables_loaded cols_loaded cleared ox16_ready xrows_ready oabs_ready yabs_ready yhat_ready mrep_ready
            largest_y largest_x ywt_ready ywt16_ready yrows_ready vmax_ready xd_ready
            xabs_ready xhat_ready yb_ready a_ready sampled samples_ready contracted ulin_ready u_ready c1_done
            zlin_ready z_ready added large_ready large_counted""".split()
        (tables_loaded, cols_loaded, cleared, ox16_ready, xrows_ready, oabs_ready,
         yabs_ready, yhat_ready, mrep_ready, largest_y, largest_x, ywt_ready, ywt16_ready, yrows_ready, vmax_ready,
         xd_ready, xabs_ready, xhat_ready, yb_ready, a_ready, sampled, samples_ready, contracted, ulin_ready, u_ready,
         c1_done, zlin_ready, z_ready, added, large_ready, large_counted) = (sem(n) for n in names)
        v_loaded = [sem(f"v_loaded{p}") for p in range(2)]
        patches_loaded = [sem(f"patches_loaded{p}") for p in range(2)]
        x_loaded = [sem(f"x_loaded{p}") for p in range(2)]
        out_stored = [sem(f"out_stored{p}") for p in range(2)]
        sp_passed, pool_passed = sem("d_sp_passed"), sem("d_pool_passed")
        block = ctx.enter_context(nc.Block())

        def pipeline(engine, iteration):
            def peeled(t):
                iteration(t, t % 2, t < NS, 1 <= t <= NS, 2 <= t <= NS + 1, 3 <= t <= NS + 2)

            for t in range(4):
                peeled(t)
            if NS > 4:
                with engine.Fori(2, NS // 2) as i:
                    for p in range(2):
                        iteration(2 * i + p, p, True, True, True, True)
            for t in range(NS, NS + 3):
                peeled(t)

        def strip(s):
            return s // PER, (s % PER) * ROWS

        @block.sync
        def _(sp):
            sp.dma_start(cols[:], tables["cols"]).then_inc(cols_loaded, 16)
            for dst, src in ((wdt[:], wd), (wct[:], wc), (selx[:], tables["selx"]),
                             (sely[:], tables["sely"].rearrange("p c y x -> p c (y x)"))):
                sp.dma_start(dst, src).then_inc(tables_loaded, 16)
            sp.wait_ge(cleared, 1)
            for p in range(2):
                sp.dma_start(xrows[p][0:2, :], tables["xpos"]).then_inc(tables_loaded, 16)

            def iteration(t, p, prep, front, back, tail):
                if prep:
                    b, y = strip(t)
                    for used in (yabs_ready, mrep_ready, xrows_ready):
                        at_least(sp, used, t - 1)
                        sp.sem_inc(sp_passed, 1)
                    for tile, row, times in ((vy[p][0:YROWS, :], V_OY, 2 * NHAT), (vm[p][0:YROWS, :], V_M, 2 * NHAT),
                                             (vx[p][X_ROW:X_ROW + 2 * GK, :], V_OX, 2)):
                        src = offsets[b, row:row + GK, bass.ds(y, ROWS), :].rearrange("c r w -> c (r w)")
                        sp.dma_start(tile, src.unsqueeze(0).to_broadcast([times, GK, N])).then_inc(v_loaded[p], 16)
                if back:
                    b, y = strip(t - 2)
                    at_least(sp, out_stored[p], 16 * ((t - 2) // 2))
                    sp.sem_inc(sp_passed, 1)
                    sp.dma_start(xres[p][:].rearrange("c (r w) -> c r w", w=W),
                                 xpad[b, :, bass.ds(y + 1, ROWS), :]).then_inc(x_loaded[p], 16)
                if prep:
                    b, y = strip(t)
                    at_least(sp, sampled, NP * (t - 1))
                    sp.sem_inc(sp_passed, 1)
                    for i in range(NP):
                        sp.dma_start(patches[p][:, i, :], hpix[b, bass.ds(y, QY), PX * i:PX * i + QX, :]
                                     ).then_inc(patches_loaded[p], 16)

            pipeline(sp, iteration)

        @block.gpsimd
        def _(pool):
            for p in range(2):
                nc.gpsimd.memset(xrows[p][:], 0.0)
            nc.gpsimd.memset(largest[:], 0.0).then_inc(cleared, 1)
            pool.wait_ge(cleared, 1)

            def iteration(t, p, prep, front, back, tail):
                q = 1 - p
                if tail:
                    b, y = strip(t - 3)
                    pool.wait_ge(z_ready, t - 2)
                    pool.wait_ge(x_loaded[q], 16 * ((t - 3) // 2 + 1))
                    nc.gpsimd.tensor_tensor(xres[q][:], z[:], xres[q][:], ALU.add).then_inc(added, 1)
                    pool.wait_ge(added, t - 2)
                    pool.dma_start(out[b, :, bass.ds(y, ROWS), :],
                                   xres[q][:].rearrange("c (r w) -> c r w", w=W)).then_inc(out_stored[q], 16)

            pipeline(pool, iteration)
            for p in range(2):
                pool.wait_ge(out_stored[p], 16 * (NS // 2))

        @block.tensor
        def _(pe):
            pe.wait_ge(tables_loaded, 16 * 6)
            pe.wait_ge(cols_loaded, 16)

            def iteration(t, p, prep, front, back, tail):
                q = 1 - p
                for j in range(K):
                    if front:
                        n = 9 * (t - 1) + j
                        if j == 0:
                            pe.wait_ge(xrows_ready, t)
                        at_least(pe, xabs_ready, n)
                        for g in range(G):
                            mm = nc.tensor.matmul(px[:, g, :], selx[:, g * K + j, :], xrows[q][:],
                                                  start=True, stop=True)
                        mm.then_inc(xd_ready, 1)
                    if back:
                        for i in PSTEP[j]:
                            if i == 0:
                                pe.wait_ge(a_ready, K * (t - 1))
                                pe.wait_ge(patches_loaded[p], 16 * NP * (t // 2))
                            at_least(pe, samples_ready, NP * (t - 2) + max(i - 2, 0))
                            w = width[i]
                            for g in range(G):
                                mm = nc.tensor.matmul(
                                    pg[i % 3][CG * g:CG * g + CG, 0:K * ROWS * w],
                                    patches[p][:, i, CG * g:CG * g + CG],
                                    A[p][:, :, g, :].rearrange("q k (r x) -> q k r x", x=W)[:, :, :, PX * i:PX * i + w],
                                    start=True, stop=True)
                            mm.then_inc(sampled, 1)
                    if tail and j == 4:
                        pe.wait_ge(u_ready, t - 2)
                        nc.tensor.matmul(po[:], wct[:], u[:], start=True, stop=True).then_inc(c1_done, 1)
                    if back and j in OSTEP:
                        for k in OSTEP[j]:
                            if k == 0:
                                pe.wait_ge(samples_ready, NP * (t - 1))
                                at_least(pe, zlin_ready, t - 2)
                            mm = nc.tensor.matmul(po[:], wdt[:, k, :], samples[:, k, :], start=(k == 0),
                                                  stop=(k == K - 1))
                        if k == K - 1:
                            mm.then_inc(contracted, 1)
                    if front:
                        at_least(pe, a_ready, n)
                        if j == 0:
                            pe.wait_ge(yrows_ready, t)
                        for g in range(G):
                            for r in range(ROWS):
                                span = slice(r * W, r * W + W)
                                window = slice((ROWS - 1 - r) * QX, (ROWS - 1 - r) * QX + 128)
                                mm = nc.tensor.matmul(py[:, g, span], sely[:, g * K + j, window], yrows[q][:, span],
                                                      start=True, stop=True)
                        mm.then_inc(yb_ready, 1)

            pipeline(pe, iteration)
            pe.wait_ge(large_ready, 1)
            nc.tensor.matmul(po[0:1, 0:1], vmax[:, 1:2], cols[:, 3:4], start=True, stop=True).then_inc(large_counted, 1)

        @block.scalar
        def _(act):
            act.wait_ge(cols_loaded, 16)

            def iteration(t, p, prep, front, back, tail):
                q = 1 - p
                for j in range(K):
                    if front:
                        n = 9 * (t - 1) + j
                        h = (j + q) % 2
                        act.wait_ge(xd_ready, n + 1)
                        at_least(act, xhat_ready, n)
                        nc.scalar.activation(xabs[:], px[:], ACT.Abs).then_inc(xabs_ready, 1)
                        act.wait_ge(xabs_ready, n + 1)
                        at_least(act, a_ready, n - 1)
                        nc.scalar.activation(xhat[h][:], xabs[:], ACT.Relu, bias=1.0, scale=-1.0
                                             ).then_inc(xhat_ready, 1)
                    if tail and j == 0:
                        act.wait_ge(contracted, t - 2)
                        at_least(act, c1_done, t - 3)
                        nc.scalar.activation(u[:], po[:], ACT.Identity, bias=bn[:, 6:7], scale=bn[:, 8:9]
                                             ).then_inc(ulin_ready, 1)
                    if tail and j == 4:
                        act.wait_ge(c1_done, t - 2)
                        at_least(act, added, t - 3)
                        nc.scalar.activation(z[:], po[:], ACT.Identity, bias=bn[:, 7:8], scale=bn[:, 3:4]
                                             ).then_inc(zlin_ready, 1)
                    if prep:
                        if j == 5:
                            act.wait_ge(v_loaded[p], V_LOADS * (t // 2 + 1))
                            at_least(act, yhat_ready, t)
                            at_least(act, largest_y, t)
                            nc.scalar.activation(yabs[:], vy[p][:], ACT.Abs, bias=cols[0:YROWS, 0:1]
                                                 ).then_inc(yabs_ready, 1)
                            act.wait_ge(yabs_ready, t + 1)
                            at_least(act, ywt_ready, t)
                            nc.scalar.activation(yhat[:], yabs[:], ACT.Relu, bias=1.0, scale=-1.0
                                                 ).then_inc(yhat_ready, 1)
                        if j == 6:
                            nc.scalar.activation(mrep[:], vm[p][:], ACT.Sigmoid).then_inc(mrep_ready, 1)
                        if j == 7:
                            x_rows = slice(X_ROW, X_ROW + 2 * GK)
                            act.wait_ge(ox16_ready, t + 1)
                            at_least(act, largest_x, t)
                            nc.scalar.activation(oabs[x_rows, :], ox16[x_rows, :], ACT.Abs).then_inc(oabs_ready, 1)
            pipeline(act, iteration)

        @block.vector
        def _(dve):
            dve.wait_ge(cols_loaded, 16)
            dve.wait_ge(cleared, 1)

            def iteration(t, p, prep, front, back, tail):
                q = 1 - p
                for j in range(K):
                    if back:
                        for i in PSTEP[j]:
                            dve.wait_ge(sampled, NP * (t - 2) + i + 1)
                            if i == 0:
                                at_least(dve, contracted, t - 2)
                            w = width[i]
                            nc.vector.tensor_copy(
                                samples[:].rearrange("c k (r x) -> c k r x", x=W)[:, :, :, PX * i:PX * i + w],
                                pg[i % 3][:, 0:K * ROWS * w].rearrange("c (k r x) -> c k r x", k=K, x=w)
                            ).then_inc(samples_ready, 1)
                    if prep and j == 4:
                        ox = slice(X_ROW, X_ROW + 2 * GK)
                        dve.wait_ge(v_loaded[p], V_LOADS * (t // 2 + 1))
                        at_least(dve, xrows_ready, t)
                        at_least(dve, oabs_ready, t)
                        nc.vector.tensor_copy(ox16[ox, :], vx[p][ox, :]).then_inc(ox16_ready, 1)
                        dve.wait_ge(ox16_ready, t + 1)
                        at_least(dve, xd_ready, K * (t - 1))
                        nc.vector.scalar_tensor_tensor(xrows[p][ox, :], ox16[ox, :], cols[ox, 2:3], vx[p][ox, :],
                                                       ALU.mult, ALU.add).then_inc(xrows_ready, 1)
                    if prep and j == 6:
                        dve.wait_ge(yabs_ready, t + 1)
                        at_least(dve, largest_y, t)
                        nc.vector.tensor_tensor(largest[0:GK, :], largest[0:GK, :], yabs[0:GK, :], ALU.max
                                                ).then_inc(largest_y, 1)
                    if prep and j == 7:
                        dve.wait_ge(mrep_ready, t + 1)
                        dve.wait_ge(yhat_ready, t + 1)
                        at_least(dve, yrows_ready, t)
                        nc.vector.scalar_tensor_tensor(ywt[:], yhat[:], MSCALE, mrep[:], ALU.mult, ALU.mult
                                                       ).then_inc(ywt_ready, 1)
                        dve.wait_ge(ywt_ready, t + 1)
                        nc.vector.tensor_copy(ywt16[:], ywt[:]).then_inc(ywt16_ready, 1)
                        dve.wait_ge(ywt16_ready, t + 1)
                        at_least(dve, yb_ready, K * (t - 1))
                        nc.vector.scalar_tensor_tensor(yrows[p][:], ywt16[:], cols[0:YROWS, 1:2], ywt[:],
                                                       ALU.mult, ALU.add).then_inc(yrows_ready, 1)
                    if prep and j == 8:
                        dve.wait_ge(oabs_ready, t + 1)
                        at_least(dve, largest_x, t)
                        x_rows = slice(X_ROW, X_ROW + 2 * GK)
                        nc.vector.tensor_tensor(largest[x_rows, :], largest[x_rows, :], oabs[x_rows, :], ALU.max
                                                ).then_inc(largest_x, 1)
                    if front:
                        n = 9 * (t - 1) + j
                        h = (j + q) % 2
                        dve.wait_ge(xhat_ready, n + 1)
                        dve.wait_ge(yb_ready, n + 1)
                        if j == 0:
                            at_least(dve, sampled, NP * (t - 2))
                        nc.vector.tensor_tensor(A[q][:, j, :, :], xhat[h][:], py[:], ALU.mult).then_inc(a_ready, 1)
                    if tail and j == 0:
                        dve.wait_ge(ulin_ready, t - 2)
                        nc.vector.scalar_tensor_tensor(u[:], u[:], SLOPE, u[:], ALU.mult, ALU.max).then_inc(u_ready, 1)
                    if tail and j == 5:
                        dve.wait_ge(zlin_ready, t - 2)
                        nc.vector.scalar_tensor_tensor(z[:], z[:], SLOPE, z[:], ALU.mult, ALU.max).then_inc(z_ready, 1)

            pipeline(dve, iteration)
            dve.wait_ge(largest_x, NS)
            dve.wait_ge(largest_y, NS)
            nc.vector.tensor_reduce(vmax[:, 0:1], largest[:], AX.X, ALU.max).then_inc(vmax_ready, 1)
            dve.wait_ge(vmax_ready, 1)
            nc.vector.tensor_scalar(vmax[:, 1:2], vmax[:, 0:1], 1.0, None, ALU.is_ge).then_inc(large_ready, 1)
            dve.wait_ge(large_counted, 1)
            nc.vector.tensor_scalar(is_large[0:1, :], po[0:1, 0:1], 1.0, None, ALU.min).then_inc(large_ready, 1)
            dve.wait_ge(large_ready, 2)


def general_block(nc, B, H, W, xpad, hpad, hpix, out, tables, wo, wo_bias, wd, wc, bn, is_large):
    assert W == 128
    WP = pixel_columns(W)
    ROWS_ALL = B * H
    with ExitStack() as ctx:
        def sb(name, shape, dt=F32):
            return ctx.enter_context(nc.sbuf_tensor(f"g_{name}", shape, dt))

        def sem(name):
            return ctx.enter_context(nc.semaphore(f"g_{name}"))

        def psum(name, shape):
            return ctx.enter_context(nc.psum_tensor(f"g_{name}", shape, F32))

        ident = sb("ident", [128, 128])
        ones = sb("ones", [1, 128])
        bias_row = sb("bias_row", [1, 128])
        wot = sb("wot", [C, K, HALF_V])
        wdt = sb("wdt", [C, K, C])
        wct = sb("wct", [C, C])
        taps = sb("taps", [128, 3, GK])
        xcol = sb("xcol", [128, 1])
        rows_h = sb("rows_h", [C, KS, W + 2])
        xrow = sb("xrow", [C, W])
        rowpos = sb("rowpos", [128, 2])
        mask = sb("mask", [128, GK])
        whole = sb("whole", [128, 2, GK], I32)
        coord = sb("coord", [128, 2, GK])
        low = sb("low", [128, 2, GK])
        work = sb("work", [128, 2, GK])
        side = sb("side", [128, 2, 2, GK])
        place = sb("place", [128, 2, 2, GK])
        cweight = sb("cweight", [128, 4, GK])
        cindex_f = sb("cindex_f", [128, 4, GK])
        cindex = sb("cindex", [128, 4, GK], I32)
        corners = sb("corners", [128, 4, GK, CG])
        sampled = sb("sampled", [128, K, G, CG])
        samples_t = sb("samples_t", [C, K, W])
        u = sb("u", [C, W])
        z = sb("z", [C, W])
        turn_ps = psum("turn_ps", [128, 3, BANK])
        offs_ps = psum("offs_ps", [128, BANK])
        out_ps = psum("out_ps", [128, BANK])

        (loaded, ready, row_in, row_free, conv_done, mask_ready, chain,
         index_ready, gathered, row_gathered, blended, turned, copied, contracted, ulin_ready, u_ready, c1_done,
         zlin_ready, row_stored) = (sem(n) for n in """loaded ready row_in row_free
         conv_done mask_ready chain index_ready gathered row_gathered blended turned copied contracted ulin_ready
         u_ready c1_done zlin_ready row_stored""".split())
        sp_passed, pool_passed = sem("sp_passed"), sem("pool_passed")
        block = ctx.enter_context(nc.Block())

        def rows(engine, body):
            with engine.Fori(0, ROWS_ALL) as t:
                body(t, t // H, t % H)

        def where_large(engine):
            return engine.If(engine.value_load(is_large[0:1, 0:1], min_val=0, max_val=1) > 0)

        @block.sync
        def _(sp):
            with where_large(sp):
                for dst, src in ((ident, tables["ident"]), (wot, wo), (wdt, wd), (wct, wc), (taps, tables["taps"]),
                                 (xcol, tables["xcol"]), (bias_row, wo_bias.rearrange("p o -> o p"))):
                    sp.dma_start(dst[:], src).then_inc(loaded, 16)

                sp.wait_ge(ready, 3)

                def body(t, b, y):
                    sp.wait_ge(row_free, t + 1)
                    sp.dma_start(rows_h[:, :, 1:W + 1], hpad[b, :, bass.ds(y + 1, KS), :]).then_inc(row_in, 16)
                    sp.dma_start(xrow[:], xpad[b, :, y + 1, :]).then_inc(row_in, 16)
                    sp.dma_start(rowpos[:], tables["rowpos"][t]).then_inc(row_in, 16)
                    sp.wait_ge(row_free, t + 2)
                    sp.dma_start(out[b, :, y, :], z[:]).then_inc(row_stored, 16)
                    sp.wait_ge(row_stored, 16 * (t + 1))
                    sp.sem_inc(sp_passed, 1)

                rows(sp, body)

        @block.gpsimd
        def _(pool):
            with where_large(pool):
                nc.gpsimd.memset(ones[:], 1.0).then_inc(ready, 1)
                nc.gpsimd.memset(rows_h[:], 0.0).then_inc(ready, 1)
                pool.wait_ge(ready, 2)
                nc.gpsimd.memset(u[:], 0.0).then_inc(ready, 1)
                pool.wait_ge(ready, 3)
                nc.gpsimd.memset(z[:], 0.0).then_inc(row_free, 1)
                table = hpix.rearrange("b y x (g c) -> (b y x g) c", g=G)

                def body(t, b, y):
                    pool.wait_ge(index_ready, t + 1)
                    pool.sem_inc(pool_passed, 1)
                    for n in range(4 * GK):
                        pool.indirect_dma_start(
                            out=corners[:].rearrange("p a c e -> p (a c) e")[:, n, :], out_offset=None, in_=table,
                            in_offset=bass.IndirectOffsetOnAxis(
                                ap=cindex[:].rearrange("p a c -> p (a c)")[:, n:n + 1], axis=0)
                        ).then_inc(gathered, 16)
                    pool.wait_ge(gathered, 16 * 4 * GK)
                    pool.dma_reset()
                    pool.sem_clear(gathered)
                    pool.sem_inc(row_gathered, 1)

                rows(pool, body)

        @block.tensor
        def _(pe):
            with where_large(pe):
                pe.wait_ge(loaded, 16 * 7)
                pe.wait_ge(ready, 3)

                def body(t, b, y):
                    pe.wait_ge(row_in, 48 * (t + 1))
                    for k in range(K):
                        nc.tensor.matmul(offs_ps[:, 0:NV], rows_h[:, k // KS, k % KS:k % KS + W], wot[:, k, 0:NV],
                                         start=(k == 0), stop=False)
                    nc.tensor.matmul(offs_ps[:, 0:NV], ones[:], bias_row[:, 0:NV], start=False, stop=True
                                     ).then_inc(conv_done, 1)
                    pe.wait_ge(blended, t + 1)
                    for k in range(K):
                        mm = nc.tensor.transpose(turn_ps[:, k // 4, (k % 4) * C:(k % 4) * C + C],
                                                 sampled[:, k].rearrange("p g c -> p (g c)"), ident[:])
                    mm.then_inc(turned, 1)
                    pe.wait_ge(copied, t + 1)
                    for k in range(K):
                        mm = nc.tensor.matmul(out_ps[:, 0:W], wdt[:, k, :], samples_t[:, k, :], start=(k == 0),
                                              stop=(k == K - 1))
                    mm.then_inc(contracted, 1)
                    pe.wait_ge(u_ready, t + 1)
                    nc.tensor.matmul(out_ps[:, 0:W], wct[:], u[:], start=True, stop=True).then_inc(c1_done, 1)

                rows(pe, body)

        @block.scalar
        def _(act):
            with where_large(act):
                def body(t, b, y):
                    act.wait_ge(conv_done, t + 1)
                    nc.scalar.activation(mask[:], offs_ps[:, V_M:V_M + GK], ACT.Sigmoid).then_inc(mask_ready, 1)
                    act.wait_ge(turned, t + 1)
                    flat = samples_t[:].rearrange("c k w -> c (k w)")
                    for r in range(3):
                        m = min(BANK, K * W - BANK * r)
                        last = nc.scalar.copy(flat[:, BANK * r:BANK * r + m], turn_ps[:, r, 0:m])
                    last.then_inc(copied, 1)
                    act.wait_ge(contracted, t + 1)
                    nc.scalar.activation(u[:], out_ps[:, 0:W], ACT.Identity, bias=bn[:, 6:7], scale=bn[:, 2:3]
                                         ).then_inc(ulin_ready, 1)
                    act.wait_ge(c1_done, t + 1)
                    nc.scalar.activation(z[:], out_ps[:, 0:W], ACT.Identity, bias=bn[:, 7:8], scale=bn[:, 3:4]
                                         ).then_inc(zlin_ready, 1)

                rows(act, body)

        @block.vector
        def _(dve):
            V = nc.vector
            STEPS = 42

            def body(t, b, y):
                n = [0]

                def link(instruction):
                    n[0] += 1
                    instruction.then_inc(chain, 1)
                    dve.wait_ge(chain, STEPS * t + n[0])

                dve.wait_ge(conv_done, t + 1)
                dve.wait_ge(row_in, 48 * (t + 1))
                dve.wait_ge(mask_ready, t + 1)
                axes = ((V_OY, rowpos[:, 0:1], H), (V_OX, xcol[:, 0:1], W))
                for a, (col, position, size) in enumerate(axes):
                    link(V.scalar_tensor_tensor(coord[:, a], offs_ps[:, col:col + GK], position, taps[:, a], ALU.add,
                                                ALU.add))
                    link(V.tensor_scalar(coord[:, a], coord[:, a], -2.0, float(size), ALU.max, ALU.min))
                link(V.tensor_copy(whole[:], coord[:]))
                link(V.tensor_copy(low[:], whole[:]))
                link(V.tensor_tensor(work[:], low[:], coord[:], ALU.is_gt))
                link(V.tensor_tensor(low[:], low[:], work[:], ALU.subtract))
                link(V.tensor_tensor(side[:, :, 1], coord[:], low[:], ALU.subtract))
                link(V.tensor_scalar(side[:, :, 0], side[:, :, 1], -1.0, 1.0, ALU.mult, ALU.add))
                link(V.tensor_copy(place[:, :, 0], low[:]))
                link(V.tensor_scalar(place[:, :, 1], low[:], 1.0, None, ALU.add))
                for a, (_, _, size) in enumerate(axes):
                    for corner in range(2):
                        p, s = place[:, a, corner], side[:, a, corner]
                        link(V.tensor_scalar(work[:, 0], p, 0.0, None, ALU.is_ge))
                        link(V.tensor_tensor(s, s, work[:, 0], ALU.mult))
                        link(V.tensor_scalar(work[:, 0], p, float(size - 1), None, ALU.is_le))
                        link(V.tensor_tensor(s, s, work[:, 0], ALU.mult))
                        link(V.tensor_scalar(p, p, 0.0, float(size - 1), ALU.max, ALU.min))
                for corner in range(2):
                    p = place[:, 0, corner]
                    link(V.tensor_scalar(p, p, float(WP * G), rowpos[:, 1:2], ALU.mult, ALU.add))
                    q = place[:, 1, corner]
                    link(V.scalar_tensor_tensor(q, q, float(G), taps[:, 2], ALU.mult, ALU.add))
                for i in range(4):
                    V.tensor_tensor(cindex_f[:, i], place[:, 0, i // 2], place[:, 1, i % 2], ALU.add)
                    last = V.tensor_tensor(cweight[:, i], side[:, 0, i // 2], side[:, 1, i % 2], ALU.mult)
                link(last)
                V.tensor_copy(cindex[:], cindex_f[:]).then_inc(index_ready, 1)
                link(V.tensor_tensor(cweight[:], cweight[:], mask[:].unsqueeze(1).to_broadcast([128, 4, GK]), ALU.mult))
                dve.wait_ge(row_gathered, t + 1)
                flat = corners[:].rearrange("p a c e -> p (a c) e")
                link(V.tensor_tensor(flat, flat, cweight[:].rearrange("p a c -> p (a c)").unsqueeze(2).to_broadcast(
                    [128, 4 * GK, CG]), ALU.mult))
                link(V.tensor_tensor(corners[:, 0], corners[:, 0], corners[:, 1], ALU.add))
                link(V.tensor_tensor(corners[:, 2], corners[:, 2], corners[:, 3], ALU.add))
                V.tensor_tensor(sampled[:].rearrange("p k g e -> p g k e"),
                                corners[:, 0].rearrange("p (g k) e -> p g k e", g=G),
                                corners[:, 2].rearrange("p (g k) e -> p g k e", g=G), ALU.add).then_inc(blended, 1)
                dve.wait_ge(ulin_ready, t + 1)
                V.scalar_tensor_tensor(u[:], u[:], SLOPE, u[:], ALU.mult, ALU.max).then_inc(u_ready, 1)
                dve.wait_ge(zlin_ready, t + 1)
                link(V.scalar_tensor_tensor(z[:], z[:], SLOPE, z[:], ALU.mult, ALU.max))
                assert n[0] == STEPS, n[0]
                V.tensor_tensor(z[:], z[:], xrow[:], ALU.add).then_inc(row_free, 1)

            with where_large(dve):
                dve.wait_ge(loaded, 16 * 7)
                rows(dve, body)


def build(nc, shape, d):
    B, _, H, W = shape
    h1pad = nc.dram_tensor("h1pad", [B, C, H + 2, W], F32).ap()
    hpad = nc.dram_tensor("hpad", [B, C, H + 4, W], F32).ap()
    offsets = nc.dram_tensor("offsets", [B, NV, H, W], F32).ap()
    hpix = nc.dram_tensor("hpix", [B, H + 4, pixel_columns(W), C], F32).ap()
    with nc.sbuf_tensor("is_large", [1, 1], I32) as is_large, nc.sbuf_tensor("chan", [C, 20], F32) as chan, \
            nc.sbuf_tensor("bn", [C, 9], F32) as bn, nc.sbuf_tensor("work", [C, 16], F32) as work:
        convolution_block(nc, B, H, W, d["xpad"], d["chan"], d["w1"], d["w2"], d["wo"], d["wo_bias"], h1pad, hpad,
                          hpix, offsets, d["ident"], chan, bn, work)
        deformable_block(nc, B, H, W, d["xpad"], hpix, offsets, d["out"], d, d["wd"], d["wc"], bn, is_large)
        general_block(nc, B, H, W, d["xpad"], hpad, hpix, d["out"], d, d["wo"], d["wo_bias"], d["wd"], d["wc"], bn,
                      is_large)


def lay_out(x, rb_w1, rb_b1, rb_bn1, rb_w2, rb_b2, rb_bn2, off_w, off_b, dc_w, dc_b, bn1, cv2_w, bn2):
    B, _, H, W = x.shape
    xpad = np.zeros((B, C, H + 2, W), np.float32)
    xpad[:, :, 1:H + 1] = x

    def taps(w):
        return np.ascontiguousarray(w.reshape(w.shape[0], C, -1).transpose(1, 2, 0))

    ow = taps(off_w)
    wo = np.zeros((C, K, HALF_V), np.float32)
    wo_bias = np.zeros((128, 1), np.float32)
    n = 2 * GK
    for row, src in ((V_OY, slice(0, n, 2)), (V_M, slice(n, n + GK)), (V_OX, slice(1, n, 2))):
        wo[:, :, row:row + GK] = ow[:, :, src]
        for half in (0, HALF_V):
            wo_bias[half + row:half + row + GK, 0] = off_b[src]
    bns = (rb_bn1, rb_bn2, bn1, bn2)
    chan = np.stack([bn[i] for i in range(4) for bn in bns] + [rb_b1, rb_b2, dc_b, np.zeros(C, np.float32)], 1)
    return dict(xpad=xpad, chan=np.ascontiguousarray(chan), w1=taps(rb_w1), w2=taps(rb_w2), wo=wo, wo_bias=wo_bias,
                wd=taps(dc_w), wc=np.ascontiguousarray(taps(cv2_w)[:, 0]), **constants(B, H, W))


def kernel(**inputs):
    import concourse.bacc as bacc
    from concourse.bass_utils import run_bass_kernel_spmd

    inputs = {name.replace("L0_conv_", ""): np.asarray(a) for name, a in inputs.items()}
    arrays = lay_out(**inputs)
    shape = inputs["x"].shape
    nc = bacc.Bacc("TRN2", target_bir_lowering=False, num_devices=1)
    d = {name: nc.dram_tensor(f"in_{name}", a.shape, mybir.dt.from_np(a.dtype), kind="ExternalInput").ap()
         for name, a in arrays.items()}
    d["out"] = nc.dram_tensor("out", shape, F32, kind="ExternalOutput").ap()
    build(nc, shape, d)
    result = run_bass_kernel_spmd(nc, [{f"in_{name}": a for name, a in arrays.items()}], core_ids=[0])
    return result.results[0]["out"]
```
